# Optimizing a Trainium2 kernel written in Bass

```python
import numpy as np
import jax
import jax.numpy as jnp

def _softmax(x, axis=-1):
    return jax.nn.softmax(x, axis=axis)

def _gelu(x):
    return jax.nn.gelu(x, approximate=True)

def _silu(x):
    return jax.nn.silu(x)

def _sigmoid(x):
    return jax.nn.sigmoid(x)

def _layernorm(x, axis=-1, eps=1e-05):
    m = jnp.mean(x, axis=axis, keepdims=True)
    v = jnp.var(x, axis=axis, keepdims=True)
    return (x - m) / jnp.sqrt(v + eps)

def _scatter_add(tgt, idx, src, axis=0):
    return tgt.at[idx].add(src)

def _segment_sum(src, seg, n):
    return jax.ops.segment_sum(src, seg, n)
kernel_name = 'mk_dlrm_tower_d1_rec_r8_be876a'

def setup_inputs(seed: int=0):
    np.random.seed(seed)
    _w = jnp.asarray

    def _rec_inputs():
        import jax
        import jax.numpy as jnp
        _tk = jax.random.key(seed)
        dense_ctx = jax.random.normal(jax.random.fold_in(_tk, 190), (2048, 16), jnp.float32)
        ids = jnp.stack([jax.random.randint(jax.random.fold_in(_tk, 200 + f), (2048,), 0, v, jnp.int32) for f, v in enumerate([1000, 1250, 1000, 12500, 1000, 1250, 1250, 12500, 1000, 12500, 12500, 12500, 1250, 1250, 12500, 1250])], axis=1)
        tbl_0 = 0.05 * jax.random.normal(jax.random.fold_in(_tk, 500 + 0), (1000, 256), jnp.float32)
        tbl_1 = 0.05 * jax.random.normal(jax.random.fold_in(_tk, 500 + 1), (1250, 256), jnp.float32)
        tbl_2 = 0.05 * jax.random.normal(jax.random.fold_in(_tk, 500 + 2), (1000, 256), jnp.float32)
        tbl_3 = 0.05 * jax.random.normal(jax.random.fold_in(_tk, 500 + 3), (12500, 256), jnp.float32)
        tbl_4 = 0.05 * jax.random.normal(jax.random.fold_in(_tk, 500 + 4), (1000, 256), jnp.float32)
        tbl_5 = 0.05 * jax.random.normal(jax.random.fold_in(_tk, 500 + 5), (1250, 256), jnp.float32)
        tbl_6 = 0.05 * jax.random.normal(jax.random.fold_in(_tk, 500 + 6), (1250, 256), jnp.float32)
        tbl_7 = 0.05 * jax.random.normal(jax.random.fold_in(_tk, 500 + 7), (12500, 256), jnp.float32)
        tbl_8 = 0.05 * jax.random.normal(jax.random.fold_in(_tk, 500 + 8), (1000, 256), jnp.float32)
        tbl_9 = 0.05 * jax.random.normal(jax.random.fold_in(_tk, 500 + 9), (12500, 256), jnp.float32)
        tbl_10 = 0.05 * jax.random.normal(jax.random.fold_in(_tk, 500 + 10), (12500, 256), jnp.float32)
        tbl_11 = 0.05 * jax.random.normal(jax.random.fold_in(_tk, 500 + 11), (12500, 256), jnp.float32)
        tbl_12 = 0.05 * jax.random.normal(jax.random.fold_in(_tk, 500 + 12), (1250, 256), jnp.float32)
        tbl_13 = 0.05 * jax.random.normal(jax.random.fold_in(_tk, 500 + 13), (1250, 256), jnp.float32)
        tbl_14 = 0.05 * jax.random.normal(jax.random.fold_in(_tk, 500 + 14), (12500, 256), jnp.float32)
        tbl_15 = 0.05 * jax.random.normal(jax.random.fold_in(_tk, 500 + 15), (1250, 256), jnp.float32)
        _rk = jax.random.fold_in(_tk, 7)
        W_top1 = 0.125 * jax.random.normal(jax.random.fold_in(_tk, 801), (64, 512), jnp.float32)
        W_top2 = 0.0441942 * jax.random.normal(jax.random.fold_in(_tk, 802), (512, 256), jnp.float32)
        W_top3 = 0.0625 * jax.random.normal(jax.random.fold_in(_tk, 803), (256, 1), jnp.float32)
        b_top1 = jnp.zeros((512,), jnp.float32)
        b_top2 = jnp.zeros((256,), jnp.float32)
        return (dense_ctx, ids, tbl_0, tbl_1, tbl_2, tbl_3, tbl_4, tbl_5, tbl_6, tbl_7, tbl_8, tbl_9, tbl_10, tbl_11, tbl_12, tbl_13, tbl_14, tbl_15, W_top1, b_top1, W_top2, b_top2, W_top3)
    dense_ctx, ids, tbl_0, tbl_1, tbl_2, tbl_3, tbl_4, tbl_5, tbl_6, tbl_7, tbl_8, tbl_9, tbl_10, tbl_11, tbl_12, tbl_13, tbl_14, tbl_15, W_top1, b_top1, W_top2, b_top2, W_top3 = _rec_inputs()

    def _L0_rec_setup():
        import jax, jax.numpy as jnp
        import numpy as np
        B, F, E = (512, 16, 256)
        N_LAYERS = 3
        key = jax.random.key(seed)
        k1, k2, k3 = jax.random.split(key, 3)
        x = jax.random.normal(k1, (B, F, E), dtype=jnp.float32)
        Ws = jax.random.normal(k2, (N_LAYERS, F, F * F), dtype=jnp.float32) * 0.05
        bs = jax.random.normal(k3, (N_LAYERS, F), dtype=jnp.float32) * 0.05
        return {'x': x, 'Ws': Ws, 'bs': bs}
    _L0_rec_all = _L0_rec_setup()
    _L0_rec_in = {k: v for k, v in _L0_rec_all.items() if k in ('Ws', 'bs')}
    del _L0_rec_all
    return {'dense_ctx': dense_ctx, 'ids': ids, 'tbl_0': tbl_0, 'tbl_1': tbl_1, 'tbl_2': tbl_2, 'tbl_3': tbl_3, 'tbl_4': tbl_4, 'tbl_5': tbl_5, 'tbl_6': tbl_6, 'tbl_7': tbl_7, 'tbl_8': tbl_8, 'tbl_9': tbl_9, 'tbl_10': tbl_10, 'tbl_11': tbl_11, 'tbl_12': tbl_12, 'tbl_13': tbl_13, 'tbl_14': tbl_14, 'tbl_15': tbl_15, 'W_top1': W_top1, 'b_top1': b_top1, 'W_top2': W_top2, 'b_top2': b_top2, 'W_top3': W_top3, 'L0_rec_Ws': _L0_rec_in['Ws'], 'L0_rec_bs': _L0_rec_in['bs']}

def reference(dense_ctx, ids, tbl_0, tbl_1, tbl_2, tbl_3, tbl_4, tbl_5, tbl_6, tbl_7, tbl_8, tbl_9, tbl_10, tbl_11, tbl_12, tbl_13, tbl_14, tbl_15, W_top1, b_top1, W_top2, b_top2, W_top3, L0_rec_Ws, L0_rec_bs):
    import jax
    import jax.numpy as jnp

    def _L0_rec_ref(x, Ws, bs):
        import jax, jax.numpy as jnp
        import numpy as np
        B, F, E = (512, 16, 256)
        N_LAYERS = 3
        B_, F_, E_ = x.shape
        n_layers = Ws.shape[0]
        xk = x
        outs = []
        for i in range(n_layers):
            z = jnp.einsum('bfe,bge->bfge', x, xk).reshape(B_, F_ * F_, E_)
            z = jnp.swapaxes(z, 1, 2)
            z = jnp.einsum('bcl,oc->bol', z, Ws[i]) + bs[i][None, :, None]
            z = jax.nn.relu(z)
            z = jnp.sum(z, axis=-1)
            outs.append(z)
            xk = jnp.broadcast_to(z[:, :, None], (B_, F_, E_))
        return jnp.concatenate(outs, axis=1)
    e = jnp.stack([tbl_0[ids[:, 0]], tbl_1[ids[:, 1]], tbl_2[ids[:, 2]], tbl_3[ids[:, 3]], tbl_4[ids[:, 4]], tbl_5[ids[:, 5]], tbl_6[ids[:, 6]], tbl_7[ids[:, 7]], tbl_8[ids[:, 8]], tbl_9[ids[:, 9]], tbl_10[ids[:, 10]], tbl_11[ids[:, 11]], tbl_12[ids[:, 12]], tbl_13[ids[:, 13]], tbl_14[ids[:, 14]], tbl_15[ids[:, 15]]], axis=1)
    z = _L0_rec_ref(e, L0_rec_Ws, L0_rec_bs)
    z = z.reshape(z.shape[0], -1)
    h = jnp.concatenate([z, dense_ctx], axis=1)
    h = jnp.maximum(h @ W_top1 + b_top1, 0.0)
    h = jnp.maximum(h @ W_top2 + b_top2, 0.0)
    y = h @ W_top3
    return y

_drawn_inputs = setup_inputs


def setup_inputs(seed=0):
    import zlib

    import numpy as np

    out = dict(_drawn_inputs(seed))
    spreads = {'b_top1': (0.0, 2.0), 'b_top2': (0.0, 2.0)}
    factors = {'dense_ctx': 8.0}
    for name, (base, spread) in spreads.items():
        noise = np.random.default_rng([zlib.crc32(name.encode()), seed]).standard_normal(out[name].shape)
        drawn = base * np.exp(spread * noise) if base else spread * noise
        out[name] = jnp.asarray(drawn.astype(out[name].dtype))
    for name, factor in factors.items():
        out[name] = (out[name] * factor).astype(out[name].dtype)
    return out
```

```python
from contextlib import ExitStack

import numpy as np
import concourse.bass as bass
from concourse import mybir

F32 = mybir.dt.float32
BF16 = mybir.dt.bfloat16
I32 = mybir.dt.int32
U32 = mybir.dt.uint32
ALU = mybir.AluOpType
ACT = mybir.ActivationFunctionType

P = 128
NF = 16
E = 256
HALVES = E // P
NL = 3
GROUPS = 4
GR = P // GROUPS
NSETS = NF // 2 + 1
SET = NF * P
DVE_SETS = 6
PROD_RING = 3
NGRP = (NSETS + 1) // 2
BANK = 512
TQ = 4
TF = NF * HALVES // TQ
PIECES = 2
PO = NF // PIECES
NTT = 2 * PIECES
NACC = 2 * NF
JUNK = 4


def build(nc, tables, ids, w0t, w12t, bias0, bias12, dense, w1, b1, w2, b2, w3,
          identity, sel_out, y_out):
    NB = ids.shape[1] // NF
    TURNS = NB // 2
    H1, H2 = w1.shape[1], w2.shape[1]
    M1, M2 = H1 // P, H2 // P
    MB = M1 + M2
    ND = dense.shape[2]
    KH = NL * NF + ND
    NQ = NB * P // BANK
    QB = BANK // P

    with ExitStack() as ctx:
        def sb(name, shape, dt=F32):
            return ctx.enter_context(nc.sbuf_tensor(name, shape, dt))

        def ps(name, shape):
            return ctx.enter_context(nc.psum_tensor(name, shape, F32))

        def sem(name):
            return ctx.enter_context(nc.semaphore(name))

        x_rows = sb("x_rows", [P, 2, NF, E])
        xt = sb("xt", [P, 2, HALVES, NF, P])
        sq = sb("sq", [P, HALVES, NF, P])
        prod = sb("prod", [P, PROD_RING, HALVES, NF, P])
        prod7 = sb("prod7", [P, HALVES, NF, P])
        prod8 = sb("prod8", [P, HALVES, NF // 2, P])
        relu0 = sb("relu0", [P, 2, 2 * BANK])
        zs_sb = sb("zs_sb", [P, BANK])
        yt_sb = sb("yt_sb", [P, BANK])
        y_sb = sb("y_sb", [P, 2, 2, NF, NF])
        outer = sb("outer", [P, PIECES, PO, NF, NF])
        junk = sb("junk", [P, JUNK, NF * NF], BF16)
        z_cur = sb("z_cur", [P, 2, NL, NF])
        z_all = sb("z_all", [P, NB, KH])
        ids_sb = sb("ids_sb", [P, NB * NF], I32)
        ids_cur = sb("ids_cur", [P, 2, NF], U32)
        w0_sb = sb("w0_sb", [P, HALVES, GR])
        w12_sb = sb("w12_sb", [P, HALVES, 2 * NF])
        bias0_sb = sb("bias0_sb", [P, 1])
        bias12_sb = sb("bias12_sb", [P, 2, NF])
        ident = sb("ident", [P, P])
        sel = sb("sel", [P, 2, GR])
        w1_sb = sb("w1_sb", [KH, H1])
        b1_sb = sb("b1_sb", [P, M1])
        w2_sb = sb("w2_sb", [P, M1, H2])
        b2_sb = sb("b2_sb", [P, M2])
        w3_sb = sb("w3_sb", [P, M2])
        y_row = sb("y_row", [1, NB * P])
        feat = prod[0:KH, 0, 0, :, :].rearrange("p f s -> p (f s)")
        h1 = x_rows[:, :, 0:M1 * BANK // E, :].rearrange("p h f e -> p h (f e)").rearrange(
            "p h (m c) -> p h m c", m=M1)
        h2 = prod7[:, :, :, :].rearrange("p h f s -> p h (f s)")[:, :, 0:M2 * BANK].rearrange(
            "p h (m c) -> p h m c", m=M2)

        z_ps = ps("z_ps", [P, 2, 2 * BANK])
        t_ps = ps("t_ps", [P, TF, P])
        zs_ps = ps("zs_ps", [P, BANK])
        turn_ps = ps("turn_ps", [P, BANK])

        setup_loaded = sem("setup_loaded")
        zeroed = sem("zeroed")
        ids_loaded = sem("ids_loaded")
        mlp_loaded = sem("mlp_loaded")
        ids_copied = sem("ids_copied")
        gathered = [sem("gathered_even"), sem("gathered_odd")]
        batches_free = sem("batches_free")
        xpose_ready = sem("xpose_ready")
        xpose_moved = sem("xpose_moved")
        dve_prod = sem("dve_prod")
        pool_prod = sem("pool_prod")
        set_done = sem("set_done")
        relu_done = sem("relu_done")
        pairs_summed = sem("pairs_summed")
        zs_moved = sem("zs_moved")
        z0_ready = sem("z0_ready")
        z0_moved = sem("z0_moved")
        yt_ready = sem("yt_ready")
        yt_moved = sem("yt_moved")
        y_ready = sem("y_ready")
        y_moved = sem("y_moved")
        outer_done = sem("outer_done")
        acc_done = sem("acc_done")
        z_stored = sem("z_stored")
        feat_ps_ready = sem("feat_ps_ready")
        feat_ready = sem("feat_ready")
        h_ready = sem("h_ready")
        h_act_done = sem("h_act_done")
        h_dve_done = sem("h_dve_done")
        out_ready = sem("out_ready")
        out_copied = sem("out_copied")
        stored = sem("stored")

        SETUP_LOADS = 5 + GROUPS
        MLP_LOADS = 6
        GATHER = 16 * NF

        block = ctx.enter_context(nc.Block())

        def done_sets(b, k):
            return NSETS * b + k + 1

        @block.sync
        def _(sp):
            sp.dma_start(ids_sb[:, :], ids).then_inc(ids_loaded, 16)
            sp.dma_start(ident[:, :], identity).then_inc(setup_loaded, 16)
            sp.dma_start(w12_sb[:, :, :], w12t.rearrange("(h p) o -> p h o", p=P)).then_inc(setup_loaded, 16)
            sp.dma_start(sel[:, :, :], sel_out).then_inc(setup_loaded, 16)
            sp.dma_start(bias12_sb[:, :, :].rearrange("p l o -> p (l o)"),
                         bias12.to_broadcast([P, 2 * NF])).then_inc(setup_loaded, 16)
            sp.wait_ge(zeroed, 2)
            sp.dma_start(w0_sb[:, :, 0:NF], w0t.rearrange("(h p) o -> p h o", p=P)).then_inc(setup_loaded, 16)
            for j in range(GROUPS):
                sp.dma_start(bias0_sb[j * GR:j * GR + NF, :], bias0).then_inc(setup_loaded, 16)
            sp.dma_start(z_all[:, :, NL * NF:KH], dense).then_inc(mlp_loaded, 16)
            sp.dma_start(w1_sb[:, :], w1).then_inc(mlp_loaded, 16)
            sp.dma_start(b1_sb[:, :], b1).then_inc(mlp_loaded, 16)
            sp.dma_start(w2_sb[:, :, :], w2.rearrange("(m p) n -> p m n", p=P)).then_inc(mlp_loaded, 16)
            sp.dma_start(b2_sb[:, :], b2).then_inc(mlp_loaded, 16)
            sp.dma_start(w3_sb[:, :], w3).then_inc(mlp_loaded, 16)
            sp.wait_ge(out_copied, NQ)
            sp.dma_start(y_out, y_row[:, :]).then_inc(stored, 16)
            sp.wait_ge(stored, 16)

        @block.gpsimd
        def _(pool):
            def gather(b, turn, par, first):
                if not first:
                    pool.wait_ge(gathered[par], GATHER * turn)
                pool.tensor_copy(ids_cur[:, par, :], ids_sb[:, bass.ds(NF * b, NF)]).then_inc(ids_copied, 1)
                if not first:
                    pool.wait_ge(xpose_ready, TQ * (b - 1))
                pool.wait_ge(ids_copied, b + 1)
                pool.sem_inc(batches_free, 1)
                for f in range(NF):
                    pool.indirect_dma_start(
                        out=x_rows[:, par, f, :], out_offset=None, in_=tables[f],
                        in_offset=bass.IndirectOffsetOnAxis(ap=ids_cur[:, par, f:f + 1], axis=0),
                    ).then_inc(gathered[par], 16)

            def products(b, par, first):
                pool.wait_ge(xpose_moved, 2 * TQ * (b + 1))
                if not first:
                    pool.wait_ge(set_done, done_sets(b - 1, 7))
                d = 7
                pool.tensor_tensor(prod7[:, :, 0:NF - d, :], xt[:, par, :, 0:NF - d, :],
                                   xt[:, par, :, d:NF, :], ALU.mult).then_inc(pool_prod, 1)
                pool.tensor_tensor(prod7[:, :, NF - d:NF, :], xt[:, par, :, NF - d:NF, :],
                                   xt[:, par, :, 0:d, :], ALU.mult).then_inc(pool_prod, 1)
                if not first:
                    pool.wait_ge(set_done, done_sets(b - 1, 8))
                d = NF // 2
                pool.tensor_tensor(prod8[:, :, :, :], xt[:, par, :, 0:d, :],
                                   xt[:, par, :, d:NF, :], ALU.mult).then_inc(pool_prod, 1)

            pool.wait_ge(ids_loaded, 16)
            gather(0, 0, 0, True)
            gather(1, 0, 1, True)
            products(0, 0, True)
            gather(2, 1, 0, False)
            products(1, 1, False)
            gather(3, 1, 1, False)
            with pool.Fori(1, TURNS - 1) as turn:
                for par in range(2):
                    products(2 * turn + par, par, False)
                    gather(2 * turn + par + 2, turn + 1, par, False)
            for par in range(2):
                products(NB - 2 + par, par, False)

        @block.scalar
        def _(act):
            act.wait_ge(setup_loaded, 16 * SETUP_LOADS)

            def move_xt(b, par, q, first):
                half, f0 = q // 2, (q % 2) * TF
                act.wait_ge(xpose_ready, TQ * b + q + 1)
                if not first and q == 0:
                    act.wait_ge(dve_prod, 2 * DVE_SETS * (b - 1))
                    act.wait_ge(pool_prod, 3 * (b - 1))
                    act.wait_ge(y_ready, b - 1)
                act.activation(xt[:, par, half, f0:f0 + TF, :], t_ps[:, :, :], ACT.Copy).then_inc(xpose_moved, 1)
                if not (isinstance(b, int) and b == 0) and q == 0:
                    act.wait_ge(set_done, done_sets(b - 1, 0))
                act.activation(sq[:, half, f0:f0 + TF, :], t_ps[:, :, :], ACT.Square).then_inc(xpose_moved, 1)

            def relu_group(b, par, g, early):
                act.wait_ge(set_done, done_sets(b, min(2 * g + 1, NSETS - 1)))
                if not early:
                    act.wait_ge(pairs_summed, NGRP * b + g - 1)
                ring = (NGRP * par + g) % 2
                n = 2 * BANK if 2 * g + 1 < NSETS else BANK // 2
                act.activation(relu0[:, ring, 0:n], z_ps[:, ring, 0:n], ACT.Relu,
                               bias=bias0_sb[:, :]).then_inc(relu_done, 1)

            def move_zs(b):
                act.wait_ge(pairs_summed, NGRP * (b + 1))
                act.activation(zs_sb[:, :], zs_ps[:, :], ACT.Copy).then_inc(zs_moved, 1)

            def move_yt(b):
                act.wait_ge(yt_ready, b + 1)
                act.activation(yt_sb[:, :], turn_ps[:, :], ACT.Copy).then_inc(yt_moved, 1)

            def move_y(b, par, first):
                act.wait_ge(y_ready, b + 1)
                if not first:
                    act.wait_ge(outer_done, NTT * (b - 1))
                act.activation(y_sb[:, par, :, :, :].rearrange("p l o (j i) -> p (l o) j i", j=GROUPS),
                               turn_ps[:, :].rearrange("p (i j c) -> p c j i", i=NF // GROUPS, j=GROUPS),
                               ACT.Copy).then_inc(y_moved, 1)

            def sum_piece(b, par, layer, piece, early):
                act.wait_ge(outer_done, NTT * b + PIECES * (layer - 1) + piece + 1)
                for i in range(PO):
                    o = PO * piece + i
                    if not (early and layer == 1 and o < JUNK):
                        act.wait_ge(acc_done, NACC * b + NF * (layer - 1) + o - JUNK + 1)
                    act.activation(junk[:, o % JUNK, :], outer[:, piece, i, :, :].rearrange("p f g -> p (f g)"),
                                   ACT.Relu, bias=bias12_sb[:, layer - 1, o:o + 1],
                                   accum_out=z_cur[:, par, layer, o:o + 1]).then_inc(acc_done, 1)

            def batch(b, par, first, early, last):
                late = not first
                if late:
                    move_zs(b - 1)
                if not last:
                    move_xt(b + 1, 1 - par, 0, first)
                relu_group(b, par, 0, first)
                if late:
                    sum_piece(b - 1, 1 - par, 1, 0, early)
                if not last:
                    move_xt(b + 1, 1 - par, 1, first)
                relu_group(b, par, 1, first)
                if late:
                    sum_piece(b - 1, 1 - par, 1, 1, early)
                move_yt(b)
                if not last:
                    move_xt(b + 1, 1 - par, 2, first)
                move_y(b, par, early)
                relu_group(b, par, 2, False)
                if late:
                    sum_piece(b - 1, 1 - par, 2, 0, early)
                if not last:
                    move_xt(b + 1, 1 - par, 3, first)
                relu_group(b, par, 3, False)
                relu_group(b, par, 4, False)
                if late:
                    sum_piece(b - 1, 1 - par, 2, 1, early)

            for q in range(TQ):
                move_xt(0, 0, q, True)
            batch(0, 0, True, True, False)
            batch(1, 1, False, True, False)
            with act.Fori(1, TURNS - 1) as turn:
                for par in range(2):
                    batch(2 * turn + par, par, False, False, False)
            batch(NB - 2, 0, False, False, False)
            batch(NB - 1, 1, False, False, True)
            move_zs(NB - 1)
            for layer in (1, 2):
                for piece in range(PIECES):
                    sum_piece(NB - 1, 1, layer, piece, False)

            act.wait_ge(mlp_loaded, 16 * MLP_LOADS)
            for q in range(NQ):
                for m in range(MB):
                    n = q * MB + m
                    if n % 2 == 0:
                        act.wait_ge(h_ready, n + 1)
                        bank = z_ps[:, (n % 4) // 2, (n % 2) * BANK:(n % 2 + 1) * BANK]
                        if m < M1:
                            act.activation(h1[:, q % 2, m, :], bank, ACT.Relu,
                                           bias=b1_sb[:, m:m + 1]).then_inc(h_act_done, 1)
                        else:
                            act.activation(h2[:, q % 2, m - M1, :], bank, ACT.Relu,
                                           bias=b2_sb[:, m - M1:m - M1 + 1]).then_inc(h_act_done, 1)

        @block.vector
        def _(dve):
            dve.memset(w0_sb[:, :, :], 0.0).then_inc(zeroed, 1)
            dve.memset(bias0_sb[:, :], 0.0).then_inc(zeroed, 1)

            def products(b, par, d, first):
                ring = (d - 1) % PROD_RING
                if d == 1:
                    dve.wait_ge(xpose_moved, 2 * TQ * (b + 1))
                if d > PROD_RING:
                    dve.wait_ge(set_done, done_sets(b, d - PROD_RING))
                elif not first:
                    dve.wait_ge(set_done, done_sets(b - 1, d + DVE_SETS - PROD_RING))
                dve.tensor_tensor(prod[:, ring, :, 0:NF - d, :], xt[:, par, :, 0:NF - d, :],
                                  xt[:, par, :, d:NF, :], ALU.mult).then_inc(dve_prod, 1)
                dve.tensor_tensor(prod[:, ring, :, NF - d:NF, :], xt[:, par, :, NF - d:NF, :],
                                  xt[:, par, :, 0:d, :], ALU.mult).then_inc(dve_prod, 1)

            def outer_piece(b, par, layer, piece, early):
                if layer == 1 and piece == 0:
                    dve.wait_ge(z0_ready, b + 1)
                    dve.tensor_copy(z_cur[:, par, 0, :], turn_ps[:, 0:NF]).then_inc(z0_moved, 1)
                    dve.wait_ge(z0_moved, b + 1)
                    dve.wait_ge(y_moved, b + 1)
                elif layer == 2 and piece == 0:
                    dve.wait_ge(acc_done, NACC * b + NF)
                if not (early and layer == 1):
                    dve.wait_ge(acc_done, NACC * b + NF * (layer - 1) + PO * (piece - 1))
                z = z_cur[:, par, layer - 1, :]
                y = y_sb[:, par, layer - 1, piece * PO:(piece + 1) * PO, :].rearrange("p o f -> p (o f)")
                dve.tensor_tensor(outer[:, piece, :, :, :].rearrange("p o f g -> p (o f) g"),
                                  y.unsqueeze(2).to_broadcast([P, PO * NF, NF]),
                                  z.unsqueeze(1).to_broadcast([P, PO * NF, NF]), ALU.mult).then_inc(outer_done, 1)

            def keep(b, par):
                dve.wait_ge(acc_done, NACC * (b + 1))
                dve.tensor_copy(z_all[:, bass.ds(b, 1), 0:NL * NF],
                                z_cur[:, par, :, :].rearrange("p l o -> p (l o)").unsqueeze(1)
                                ).then_inc(z_stored, 1)

            def batch(b, par, first, early):
                late = not first
                products(b, par, 1, first)
                if late and not early:
                    keep(b - 2, par)
                products(b, par, 2, first)
                if late:
                    outer_piece(b - 1, 1 - par, 1, 0, early)
                products(b, par, 3, first)
                if late:
                    outer_piece(b - 1, 1 - par, 1, 1, early)
                products(b, par, 4, first)
                products(b, par, 5, first)
                if late:
                    outer_piece(b - 1, 1 - par, 2, 0, early)
                products(b, par, 6, first)
                if late:
                    outer_piece(b - 1, 1 - par, 2, 1, early)

            batch(0, 0, True, True)
            batch(1, 1, False, True)
            with dve.Fori(1, TURNS) as turn:
                for par in range(2):
                    batch(2 * turn + par, par, False, False)
            keep(NB - 2, 0)
            for layer in (1, 2):
                for piece in range(PIECES):
                    outer_piece(NB - 1, 1, layer, piece, False)
            keep(NB - 1, 1)

            for q in range(NQ):
                dve.wait_ge(feat_ps_ready, q + 1)
                dve.tensor_copy(feat[:, q * BANK:(q + 1) * BANK],
                                t_ps[0:KH, (q % 2) * QB:(q % 2 + 1) * QB, :].rearrange("p b s -> p (b s)")
                                ).then_inc(feat_ready, 1)
            dve.wait_ge(mlp_loaded, 16 * MLP_LOADS)
            for q in range(NQ):
                for m in range(MB):
                    n = q * MB + m
                    if n % 2:
                        dve.wait_ge(h_ready, n + 1)
                        bank = z_ps[:, (n % 4) // 2, (n % 2) * BANK:(n % 2 + 1) * BANK]
                        dst, bia = ((h1[:, q % 2, m, :], b1_sb[:, m:m + 1]) if m < M1 else
                                    (h2[:, q % 2, m - M1, :], b2_sb[:, m - M1:m - M1 + 1]))
                        dve.tensor_scalar(dst, bank, bia, 0.0, ALU.add, ALU.max).then_inc(h_dve_done, 1)
                dve.wait_ge(out_ready, q + 1)
                dve.tensor_copy(y_row[0:1, q * BANK:(q + 1) * BANK],
                                (zs_ps if q % 2 else turn_ps)[0:1, :]
                                ).then_inc(out_copied, 1)

        @block.tensor
        def _(pe):
            pe.wait_ge(setup_loaded, 16 * SETUP_LOADS)

            def transposes(b, turn, par, q, first):
                half, f0 = q // 2, (q % 2) * TF
                if q == 0:
                    pe.wait_ge(gathered[par], GATHER * (turn + 1))
                if not (first and q == 0):
                    pe.wait_ge(xpose_moved, 2 * (TQ * b + q))
                for i in range(TF):
                    mm = pe.transpose(t_ps[:, i, :], x_rows[:, par, f0 + i, half * P:(half + 1) * P], ident[:, :])
                mm.then_inc(xpose_ready, 1)

            def form_yt(b, par, first):
                if not first:
                    pe.wait_ge(z0_moved, b)
                for half in range(HALVES):
                    for j in range(GROUPS):
                        mm = pe.matmul(turn_ps[j * GR:(j + 1) * GR, :], w12_sb[:, half, :],
                                       xt[:, par, half, j * GROUPS:(j + 1) * GROUPS, :],
                                       start=(half == 0), stop=(half == HALVES - 1))
                mm.then_inc(yt_ready, 1)

            def form_y(b):
                pe.wait_ge(yt_moved, b + 1)
                for i in range(NF // GROUPS):
                    mm = pe.transpose(turn_ps[:, i * P:(i + 1) * P], yt_sb[:, i * P:(i + 1) * P], ident[:, :])
                mm.then_inc(y_ready, 1)

            def form_z0(b):
                pe.wait_ge(zs_moved, b + 1)
                pe.wait_ge(y_moved, b + 1)
                for i in range(BANK // P):
                    mm = pe.matmul(turn_ps[:, 0:NF], zs_sb[:, i * P:(i + 1) * P], sel[:, 0, 0:NF],
                                   start=(i == 0), stop=(i == BANK // P - 1))
                mm.then_inc(z0_ready, 1)

            def contract(b, par, k, first):
                ring = (NGRP * par + k // 2) % 2
                if k % 2 == 0 and not (first and k < 4):
                    pe.wait_ge(relu_done, NGRP * b + k // 2 - 1)
                if k == 0:
                    pe.wait_ge(xpose_moved, 2 * TQ * (b + 1))
                elif k <= DVE_SETS:
                    pe.wait_ge(dve_prod, 2 * DVE_SETS * b + 2 * k)
                elif k == 7:
                    pe.wait_ge(pool_prod, 3 * b + 2)
                elif k == 8:
                    pe.wait_ge(pool_prod, 3 * b + 3)
                src = (sq[:, :, :, :] if k == 0 else prod7[:, :, :, :] if k == 7 else
                       prod8[:, :, :, :] if k == 8 else prod[:, (k - 1) % PROD_RING, :, :, :])
                pairs = (NF // 2 if k == 8 else NF) // GROUPS
                col = (k % 2) * BANK
                for half in range(HALVES):
                    for j in range(GROUPS):
                        mm = pe.matmul(z_ps[j * GR:(j + 1) * GR, ring, col:col + pairs * P], w0_sb[:, half, :],
                                       src[:, half, j * pairs:(j + 1) * pairs, :],
                                       start=(half == 0), stop=(half == HALVES - 1))
                mm.then_inc(set_done, 1)

            def sum_pairs(b, par, g, first):
                ring = (NGRP * par + g) % 2
                pe.wait_ge(relu_done, NGRP * b + g + 1)
                if g == 0 and not first:
                    pe.wait_ge(zs_moved, b)
                for k in range(2 * g, min(2 * g + 2, NSETS)):
                    n = BANK if k < NSETS - 1 else BANK // 2
                    j = k % GROUPS
                    mm = pe.matmul(zs_ps[j * GR:(j + 1) * GR, 0:n],
                                   sel[:, 0 if k == 0 else 1, :],
                                   relu0[:, ring, (k % 2) * BANK:(k % 2) * BANK + n],
                                   start=(k < GROUPS), stop=(k + GROUPS >= NSETS), skip_group_check=True)
                mm.then_inc(pairs_summed, 1)

            def batch(b, turn, par, first, last):
                for k in range(NSETS):
                    if k in (2, 4, 6):
                        sum_pairs(b, par, k // 2 - 1, first)
                    contract(b, par, k, first)
                    if k == 0 and not first:
                        sum_pairs(b - 1, 1 - par, NGRP - 1, False)
                    if k % 2 == 0 and k // 2 < TQ and not last:
                        transposes(b + 1, turn + par, 1 - par, k // 2, False)
                    if k == 1 and not first:
                        form_z0(b - 1)
                    if k == 3:
                        form_yt(b, par, first)
                    if k == 4:
                        form_y(b)
                sum_pairs(b, par, NGRP - 2, first)

            for q in range(TQ):
                transposes(0, 0, 0, q, True)
            batch(0, 0, 0, True, False)
            batch(1, 0, 1, False, False)
            with pe.Fori(1, TURNS - 1) as turn:
                for par in range(2):
                    batch(2 * turn + par, turn, par, False, False)
            batch(NB - 2, TURNS - 1, 0, False, False)
            batch(NB - 1, TURNS - 1, 1, False, True)
            sum_pairs(NB - 1, 1, NGRP - 1, False)
            form_z0(NB - 1)

            pe.wait_ge(mlp_loaded, 16 * MLP_LOADS)
            pe.wait_ge(z_stored, NB)
            for q in range(NQ):
                if q >= 2:
                    pe.wait_ge(feat_ready, q - 1)
                for i in range(QB):
                    mm = pe.transpose(t_ps[0:KH, (q % 2) * QB + i, :], z_all[:, q * QB + i, :], ident[:, :])
                mm.then_inc(feat_ps_ready, 1)

            def both_done(n):
                pe.wait_ge(h_act_done, (n + 1) // 2)
                if n // 2:
                    pe.wait_ge(h_dve_done, n // 2)

            for q in range(NQ):
                pe.wait_ge(feat_ready, q + 1)
                for m in range(MB):
                    n = q * MB + m
                    if m == M1:
                        both_done(q * MB + M1)
                    elif n >= 4:
                        both_done(n - 3)
                    bank = z_ps[:, (n % 4) // 2, (n % 2) * BANK:(n % 2 + 1) * BANK]
                    if m < M1:
                        mm = pe.matmul(bank, w1_sb[:, m * P:(m + 1) * P], feat[:, q * BANK:(q + 1) * BANK],
                                       start=True, stop=True)
                    else:
                        for k in range(M1):
                            mm = pe.matmul(bank, w2_sb[:, k, (m - M1) * P:(m - M1 + 1) * P],
                                           h1[:, q % 2, k, :], start=(k == 0), stop=(k == M1 - 1))
                    mm.then_inc(h_ready, 1)
                both_done((q + 1) * MB)
                if q >= 2:
                    pe.wait_ge(out_copied, q - 1)
                for k in range(M2):
                    mm = pe.matmul((zs_ps if q % 2 else turn_ps)[0:1, :],
                                   w3_sb[:, k:k + 1], h2[:, q % 2, k, :], start=(k == 0), stop=(k == M2 - 1))
                mm.then_inc(out_ready, 1)


def kernel(**inputs):
    import concourse.bacc as bacc
    from concourse.bass_utils import run_bass_kernel_spmd as run

    a = {k: np.asarray(v) for k, v in inputs.items()}
    n = a["ids"].shape[0]
    nb = n // P
    ws = a["L0_rec_Ws"]
    bs = a["L0_rec_bs"]
    sel = np.zeros((GROUPS, GR, 2, GR), np.float32)
    for o in range(NF):
        sel[:, o, 0, o] = 1.0
        sel[:, o, 1, o] = 2.0
    arrays = {f"tbl_{f}": a[f"tbl_{f}"] for f in range(NF)}
    arrays |= {
        "ids": a["ids"].reshape(nb, P, NF).transpose(1, 0, 2).reshape(P, nb * NF),
        "w0t": ws[0].T,
        "w12t": ws[1:].reshape(2 * NF, E).T,
        "bias0": bs[0].reshape(NF, 1),
        "bias12": bs[1:].reshape(1, 2 * NF),
        "dense": a["dense_ctx"].reshape(nb, P, -1).transpose(1, 0, 2),
        "w1": a["W_top1"],
        "b1": a["b_top1"].reshape(-1, P).T,
        "w2": a["W_top2"],
        "b2": a["b_top2"].reshape(-1, P).T,
        "w3": a["W_top3"].reshape(-1, P).T,
        "identity": np.eye(P, dtype=np.float32),
        "sel_out": sel.reshape(P, 2, GR),
    }
    arrays = {k: np.ascontiguousarray(v) for k, v in arrays.items()}
    nc = bacc.Bacc("TRN2", target_bir_lowering=False, num_devices=1)
    args = [nc.dram_tensor(f"in_{k}", v.shape, mybir.dt.from_np(v.dtype), kind="ExternalInput").ap()
            for k, v in arrays.items()]
    out = nc.dram_tensor("out_y", (1, n), F32, kind="ExternalOutput").ap()
    build(nc, args[:NF], *args[NF:], out)
    r = run(nc, [{f"in_{k}": v for k, v in arrays.items()}], core_ids=[0])
    return r.results[0]["out_y"].reshape(n, 1)
```

```python
from contextlib import ExitStack

import numpy as np
import concourse.bass as bass
from concourse import mybir

F32 = mybir.dt.float32
BF16 = mybir.dt.bfloat16
I32 = mybir.dt.int32
U32 = mybir.dt.uint32
ALU = mybir.AluOpType
ACT = mybir.ActivationFunctionType

P = 128
NF = 16
E = 256
HALVES = E // P
NL = 3
GROUPS = 4
GR = P // GROUPS
NSETS = NF // 2 + 1
SET = NF * P
DVE_SETS = 6
NDVE = 2 * DVE_SETS - 1
NPOOL = 4
PROD_RING = 3
NGRP = (NSETS + 1) // 2
BANK = 512
TQ = 4
XPOSE_AT = (0, 2, 4, 5)
TF = NF * HALVES // TQ
PIECES = 2
PO = NF // PIECES
NTT = 2 * PIECES
NACC = 2 * NF
JUNK = 4


def build(nc, tables, ids, w0t, w12t, bias0, bias12, dense, w1, b1, w2, b2, w3,
          identity, sel_out, y_out):
    NB = ids.shape[1] // NF
    TURNS = NB // 2
    H1, H2 = w1.shape[1], w2.shape[1]
    M1, M2 = H1 // P, H2 // P
    MB = M1 + M2
    ND = dense.shape[2]
    KH = NL * NF + ND
    MC = 2 * P

    with ExitStack() as ctx:
        def sb(name, shape, dt=F32):
            return ctx.enter_context(nc.sbuf_tensor(name, shape, dt))

        def ps(name, shape):
            return ctx.enter_context(nc.psum_tensor(name, shape, F32))

        def sem(name):
            return ctx.enter_context(nc.semaphore(name))

        x_rows = sb("x_rows", [P, 2, NF, E])
        xt = sb("xt", [P, 2, HALVES, NF, P])
        sq = sb("sq", [P, HALVES, NF, P])
        prod = sb("prod", [P, PROD_RING, HALVES, NF, P])
        prod7 = sb("prod7", [P, HALVES, NF, P])
        prod8 = sb("prod8", [P, HALVES, NF // 2, P])
        relu0 = sb("relu0", [P, 2, 2 * BANK])
        zs_sb = sb("zs_sb", [P, BANK])
        yt_sb = sb("yt_sb", [P, BANK])
        y_sb = sb("y_sb", [P, 2, 2, NF, NF])
        outer = sb("outer", [P, PIECES, PO, NF, NF])
        junk = sb("junk", [P, JUNK, NF * NF], BF16)
        z_cur = sb("z_cur", [P, 2, NL, NF])
        dense_sb = sb("dense_sb", [P, NB, ND])
        cat = sb("cat", [P, 2, P])
        feat = sb("feat", [KH, MC])
        h1 = sb("h1", [P, M1, MC])
        h2 = sb("h2", [P, M2, MC])
        y_row = sb("y_row", [1, MC])
        ids_sb = sb("ids_sb", [P, NB * NF], I32)
        ids_cur = sb("ids_cur", [P, 2, NF], U32)
        w0_sb = sb("w0_sb", [P, HALVES, GR])
        w12_sb = sb("w12_sb", [P, HALVES, 2 * NF])
        bias0_sb = sb("bias0_sb", [P, 1])
        bias12_sb = sb("bias12_sb", [P, 2, NF])
        ident = sb("ident", [P, P])
        sel = sb("sel", [P, 2, GR])
        w1_sb = sb("w1_sb", [KH, H1])
        b1_sb = sb("b1_sb", [P, M1])
        w2_sb = sb("w2_sb", [P, M1, H2])
        b2_sb = sb("b2_sb", [P, M2])
        w3_sb = sb("w3_sb", [P, M2])

        z_ps = ps("z_ps", [P, 2, 2 * BANK])
        t_ps = ps("t_ps", [P, TF, P])
        zs_ps = ps("zs_ps", [P, BANK])
        turn_ps = ps("turn_ps", [P, BANK])

        setup_loaded = sem("setup_loaded")
        zeroed = sem("zeroed")
        ids_loaded = sem("ids_loaded")
        mlp_loaded = sem("mlp_loaded")
        ids_copied = sem("ids_copied")
        gathered = [[sem(f"gathered{par}{half}") for half in range(2)] for par in range(2)]
        batches_free = sem("batches_free")
        xpose_ready = sem("xpose_ready")
        xpose_moved = sem("xpose_moved")
        first_squared = sem("first_squared")
        dve_prod = sem("dve_prod")
        pool_prod = sem("pool_prod")
        set_done = sem("set_done")
        relu_done = sem("relu_done")
        pairs_summed = sem("pairs_summed")
        zs_moved = sem("zs_moved")
        z0_ready = sem("z0_ready")
        z0_moved = sem("z0_moved")
        yt_ready = sem("yt_ready")
        yt_moved = sem("yt_moved")
        y_ready = sem("y_ready")
        y_moved = sem("y_moved")
        outer_done = sem("outer_done")
        acc_done = sem("acc_done")
        z_stored = sem("z_stored")
        feat_ps_ready = sem("feat_ps_ready")
        feat_ready = sem("feat_ready")
        h_ready = sem("h_ready")
        h_done = sem("h_done")
        out_ready = sem("out_ready")
        out_copied = sem("out_copied")
        stored = sem("stored")

        SETUP_LOADS = 5 + GROUPS
        MLP_LOADS = 6
        GATHER = 16 * NF // 2

        block = ctx.enter_context(nc.Block())

        def mlp_ps(m):
            if m < M1:
                return t_ps[:, 2 * m:2 * m + 2, :].rearrange("p i s -> p (i s)")
            return turn_ps[:, (m % 2) * MC:(m % 2 + 1) * MC]

        def first_ps(q):
            return t_ps[:, :, :] if q in (0, 3) else z_ps[:, q - 1, :].rearrange("p (f s) -> p f s", f=TF)

        def done_sets(b, k):
            return NSETS * b + k + 1

        @block.sync
        def _(sp):
            sp.dma_start(ids_sb[:, :], ids).then_inc(ids_loaded, 16)
            sp.dma_start(ident[:, :], identity).then_inc(setup_loaded, 16)
            sp.dma_start(w12_sb[:, :, :], w12t.rearrange("(h p) o -> p h o", p=P)).then_inc(setup_loaded, 16)
            sp.dma_start(sel[:, :, :], sel_out).then_inc(setup_loaded, 16)
            sp.dma_start(bias12_sb[:, :, :].rearrange("p l o -> p (l o)"),
                         bias12.to_broadcast([P, 2 * NF])).then_inc(setup_loaded, 16)
            sp.wait_ge(zeroed, 2)
            sp.dma_start(w0_sb[:, :, 0:NF], w0t.rearrange("(h p) o -> p h o", p=P)).then_inc(setup_loaded, 16)
            for j in range(GROUPS):
                sp.dma_start(bias0_sb[j * GR:j * GR + NF, :], bias0).then_inc(setup_loaded, 16)
            sp.dma_start(dense_sb[:, :, :], dense).then_inc(mlp_loaded, 16)
            sp.dma_start(w1_sb[:, :], w1).then_inc(mlp_loaded, 16)
            sp.dma_start(b1_sb[:, :], b1).then_inc(mlp_loaded, 16)
            sp.dma_start(w2_sb[:, :, :], w2.rearrange("(m p) n -> p m n", p=P)).then_inc(mlp_loaded, 16)
            sp.dma_start(b2_sb[:, :], b2).then_inc(mlp_loaded, 16)
            sp.dma_start(w3_sb[:, :], w3).then_inc(mlp_loaded, 16)
            with sp.Fori(0, TURNS) as turn:
                sp.wait_ge(out_copied, turn + 1)
                sp.dma_start(y_out[:, bass.ds(MC * turn, MC)], y_row[:, :]).then_inc(stored, 16)
            sp.wait_ge(stored, 16 * TURNS)

        @block.gpsimd
        def _(pool):
            def products_wrap(b, par, first):
                d = DVE_SETS
                pool.wait_ge(set_done, done_sets(b, d - PROD_RING))
                pool.tensor_tensor(prod[:, (d - 1) % PROD_RING, :, NF - d:NF, :], xt[:, par, :, NF - d:NF, :],
                                   xt[:, par, :, 0:d, :], ALU.mult).then_inc(pool_prod, 1)
                pool.sem_inc(batches_free, 1)

            def gather(b, turn, par, first, wrap=None):
                if not first:
                    pool.wait_ge(gathered[par][0], GATHER * turn)
                    pool.wait_ge(gathered[par][1], GATHER * turn)
                pool.tensor_copy(ids_cur[:, par, :], ids_sb[:, bass.ds(NF * b, NF)]).then_inc(ids_copied, 1)
                if not first:
                    pool.wait_ge(xpose_ready, TQ * (b - 1))
                pool.wait_ge(ids_copied, b + 1)
                pool.sem_inc(batches_free, 1)
                for f in range(NF):
                    if f == NF // 2 and wrap is not None:
                        products_wrap(*wrap)
                    pool.indirect_dma_start(
                        out=x_rows[:, par, f, :], out_offset=None, in_=tables[f],
                        in_offset=bass.IndirectOffsetOnAxis(ap=ids_cur[:, par, f:f + 1], axis=0),
                    ).then_inc(gathered[par][f // (NF // 2)], 16)

            def products(b, par, first):
                pool.wait_ge(xpose_moved, TQ * (2 * b + 1))
                if not first:
                    pool.wait_ge(set_done, done_sets(b - 1, 7))
                d = 7
                pool.tensor_tensor(prod7[:, :, 0:NF - d, :], xt[:, par, :, 0:NF - d, :],
                                   xt[:, par, :, d:NF, :], ALU.mult).then_inc(pool_prod, 1)
                pool.tensor_tensor(prod7[:, :, NF - d:NF, :], xt[:, par, :, NF - d:NF, :],
                                   xt[:, par, :, 0:d, :], ALU.mult).then_inc(pool_prod, 1)
                if not first:
                    pool.wait_ge(set_done, done_sets(b - 1, 8))
                d = NF // 2
                pool.tensor_tensor(prod8[:, :, :, :], xt[:, par, :, 0:d, :],
                                   xt[:, par, :, d:NF, :], ALU.mult).then_inc(pool_prod, 1)

            pool.wait_ge(ids_loaded, 16)
            gather(0, 0, 0, True)
            gather(1, 0, 1, True)
            products(0, 0, True)
            gather(2, 1, 0, False, wrap=(0, 0, True))
            products(1, 1, False)
            gather(3, 1, 1, False, wrap=(1, 1, False))
            with pool.Fori(1, TURNS - 1) as turn:
                for par in range(2):
                    products(2 * turn + par, par, False)
                    gather(2 * turn + par + 2, turn + 1, par, False, wrap=(2 * turn + par, par, False))
            for par in range(2):
                products(NB - 2 + par, par, False)
                products_wrap(NB - 2 + par, par, False)

        @block.scalar
        def _(act):
            act.wait_ge(setup_loaded, 16 * SETUP_LOADS)

            def move_xt(b, par, q, first):
                half, f0 = q % 2, (q // 2) * TF
                act.wait_ge(xpose_ready, TQ * b + q + 1)
                if not first and q == 0:
                    act.wait_ge(dve_prod, NDVE * (b - 1))
                    act.wait_ge(pool_prod, NPOOL * (b - 1))
                    act.wait_ge(y_ready, b - 1)
                act.activation(xt[:, par, half, f0:f0 + TF, :], t_ps[:, :, :], ACT.Copy).then_inc(xpose_moved, 1)
                if q == 0:
                    act.wait_ge(set_done, done_sets(b - 1, 0))
                act.activation(sq[:, half, f0:f0 + TF, :], t_ps[:, :, :], ACT.Square).then_inc(xpose_moved, 1)

            def relu_group(b, par, g, early):
                act.wait_ge(set_done, done_sets(b, min(2 * g + 1, NSETS - 1)))
                if not early:
                    act.wait_ge(pairs_summed, NGRP * b + g - 1)
                ring = (NGRP * par + g) % 2
                n = 2 * BANK if 2 * g + 1 < NSETS else BANK // 2
                act.activation(relu0[:, ring, 0:n], z_ps[:, ring, 0:n], ACT.Relu,
                               bias=bias0_sb[:, :]).then_inc(relu_done, 1)

            def move_zs(b):
                act.wait_ge(pairs_summed, NGRP * (b + 1))
                act.activation(zs_sb[:, :], zs_ps[:, :], ACT.Copy).then_inc(zs_moved, 1)

            def move_yt(b):
                act.wait_ge(yt_ready, b + 1)
                act.activation(yt_sb[:, :], turn_ps[:, :], ACT.Copy).then_inc(yt_moved, 1)

            def move_y(b, par, first):
                act.wait_ge(y_ready, b + 1)
                if not first:
                    act.wait_ge(outer_done, NTT * (b - 1))
                act.activation(y_sb[:, par, :, :, :].rearrange("p l o (j i) -> p (l o) j i", j=GROUPS),
                               turn_ps[:, :].rearrange("p (i j c) -> p c j i", i=NF // GROUPS, j=GROUPS),
                               ACT.Copy).then_inc(y_moved, 1)

            def sum_piece(b, par, layer, piece, early):
                act.wait_ge(outer_done, NTT * b + PIECES * (layer - 1) + piece + 1)
                for i in range(PO):
                    o = PO * piece + i
                    if not (early and layer == 1 and o < JUNK):
                        act.wait_ge(acc_done, NACC * b + NF * (layer - 1) + o - JUNK + 1)
                    act.activation(junk[:, o % JUNK, :], outer[:, piece, i, :, :].rearrange("p f g -> p (f g)"),
                                   ACT.Relu, bias=bias12_sb[:, layer - 1, o:o + 1],
                                   accum_out=z_cur[:, par, layer, o:o + 1]).then_inc(acc_done, 1)

            def mlp_input(t):
                act.wait_ge(feat_ps_ready, t + 1)
                act.activation(feat[:, :], turn_ps[0:KH, 0:MC], ACT.Copy).then_inc(feat_ready, 1)

            def mlp_relu(t, m):
                if m % 2 == 0:
                    act.wait_ge(h_ready, MB // 2 * t + m // 2 + 1)
                src = mlp_ps(m)
                if m < M1:
                    act.activation(h1[:, m, :], src, ACT.Relu, bias=b1_sb[:, m:m + 1]).then_inc(h_done, 1)
                else:
                    act.activation(h2[:, m - M1, :], src, ACT.Relu,
                                   bias=b2_sb[:, m - M1:m - M1 + 1]).then_inc(h_done, 1)

            def mlp_output(t, first):
                act.wait_ge(out_ready, t + 1)
                if not first:
                    act.wait_ge(stored, 16 * t)
                act.activation(y_row[:, :], turn_ps[0:1, 0:MC], ACT.Copy).then_inc(out_copied, 1)

            def batch(b, par, first, early, last, mlp=None):
                late = not first
                if late:
                    move_zs(b - 1)
                if not last:
                    move_xt(b + 1, 1 - par, 0, first)
                relu_group(b, par, 0, first)
                if late:
                    sum_piece(b - 1, 1 - par, 1, 0, early)
                if not last:
                    move_xt(b + 1, 1 - par, 1, first)
                relu_group(b, par, 1, first)
                if late:
                    sum_piece(b - 1, 1 - par, 1, 1, early)
                move_yt(b)
                if not last:
                    move_xt(b + 1, 1 - par, 2, first)
                move_y(b, par, early)
                relu_group(b, par, 2, False)
                if not last:
                    move_xt(b + 1, 1 - par, 3, first)
                if mlp:
                    mlp_input(mlp[0])
                if late:
                    sum_piece(b - 1, 1 - par, 2, 0, early)
                if mlp:
                    for m in range(M1):
                        mlp_relu(mlp[0], m)
                relu_group(b, par, 3, False)
                if mlp:
                    for m in range(M1, MB):
                        mlp_relu(mlp[0], m)
                relu_group(b, par, 4, False)
                if mlp:
                    mlp_output(*mlp)
                if late:
                    sum_piece(b - 1, 1 - par, 2, 1, early)

            for q in range(TQ):
                half, f0 = q % 2, (q // 2) * TF
                act.wait_ge(xpose_ready, q + 1)
                act.activation(xt[:, 0, half, f0:f0 + TF, :], first_ps(q), ACT.Copy).then_inc(xpose_moved, 1)
            batch(0, 0, True, True, False)
            batch(1, 1, False, True, False)
            act.wait_ge(mlp_loaded, 16 * MLP_LOADS)
            batch(2, 0, False, False, False)
            batch(3, 1, False, False, False, mlp=(0, True))
            with act.Fori(2, TURNS - 1) as turn:
                batch(2 * turn, 0, False, False, False)
                batch(2 * turn + 1, 1, False, False, False, mlp=(turn - 1, False))
            batch(NB - 2, 0, False, False, False)
            batch(NB - 1, 1, False, False, True, mlp=(TURNS - 2, False))
            move_zs(NB - 1)
            for layer in (1, 2):
                for piece in range(PIECES):
                    sum_piece(NB - 1, 1, layer, piece, False)
            mlp_input(TURNS - 1)
            for m in range(MB):
                mlp_relu(TURNS - 1, m)
            mlp_output(TURNS - 1, False)

        @block.vector
        def _(dve):
            dve.memset(w0_sb[:, :, :], 0.0).then_inc(zeroed, 1)
            dve.memset(bias0_sb[:, :], 0.0).then_inc(zeroed, 1)
            dve.memset(cat[:, :, KH:P], 0.0).then_inc(zeroed, 1)

            def products(b, par, d, first):
                ring = (d - 1) % PROD_RING
                if d == 1:
                    dve.wait_ge(xpose_moved, TQ * (2 * b + 1))
                if d > PROD_RING:
                    dve.wait_ge(set_done, done_sets(b, d - PROD_RING))
                elif not first:
                    dve.wait_ge(set_done, done_sets(b - 1, d + DVE_SETS - PROD_RING))
                dve.tensor_tensor(prod[:, ring, :, 0:NF - d, :], xt[:, par, :, 0:NF - d, :],
                                  xt[:, par, :, d:NF, :], ALU.mult).then_inc(dve_prod, 1)
                if d < DVE_SETS:
                    dve.tensor_tensor(prod[:, ring, :, NF - d:NF, :], xt[:, par, :, NF - d:NF, :],
                                      xt[:, par, :, 0:d, :], ALU.mult).then_inc(dve_prod, 1)

            def outer_piece(b, par, layer, piece, early):
                if layer == 1 and piece == 0:
                    dve.wait_ge(z0_ready, b + 1)
                    dve.tensor_copy(z_cur[:, par, 0, :], turn_ps[:, 0:NF]).then_inc(z0_moved, 1)
                    dve.wait_ge(z0_moved, b + 1)
                    dve.wait_ge(y_moved, b + 1)
                elif layer == 2 and piece == 0:
                    dve.wait_ge(acc_done, NACC * b + NF)
                if not (early and layer == 1):
                    dve.wait_ge(acc_done, NACC * b + NF * (layer - 1) + PO * (piece - 1))
                z = z_cur[:, par, layer - 1, :]
                y = y_sb[:, par, layer - 1, piece * PO:(piece + 1) * PO, :].rearrange("p o f -> p (o f)")
                dve.tensor_tensor(outer[:, piece, :, :, :].rearrange("p o f g -> p (o f) g"),
                                  y.unsqueeze(2).to_broadcast([P, PO * NF, NF]),
                                  z.unsqueeze(1).to_broadcast([P, PO * NF, NF]), ALU.mult).then_inc(outer_done, 1)

            def keep(b, turn, par, early):
                dve.wait_ge(acc_done, NACC * (b + 1))
                if not early:
                    dve.wait_ge(feat_ps_ready, turn)
                dve.tensor_copy(cat[:, par, 0:NL * NF],
                                z_cur[:, par, :, :].rearrange("p l o -> p (l o)")).then_inc(z_stored, 1)
                dve.tensor_copy(cat[:, par, NL * NF:KH].unsqueeze(1), dense_sb[:, bass.ds(b, 1), :]
                                ).then_inc(z_stored, 1)

            def batch(b, turn, par, first, early):
                late = not first
                products(b, par, 1, first)
                if late and not early:
                    keep(b - 2, turn - 1, par, isinstance(turn, int) and turn == 1)
                products(b, par, 2, first)
                if late:
                    outer_piece(b - 1, 1 - par, 1, 0, early)
                products(b, par, 3, first)
                if late:
                    outer_piece(b - 1, 1 - par, 1, 1, early)
                products(b, par, 4, first)
                products(b, par, 5, first)
                if late:
                    outer_piece(b - 1, 1 - par, 2, 0, early)
                products(b, par, 6, first)
                if late:
                    outer_piece(b - 1, 1 - par, 2, 1, early)

            for q in range(TQ):
                half, f0 = q % 2, (q // 2) * TF
                dve.wait_ge(xpose_moved, q + 1)
                x = xt[:, 0, half, f0:f0 + TF, :]
                dve.tensor_tensor(sq[:, half, f0:f0 + TF, :], x, x, ALU.mult).then_inc(first_squared, 1)
            batch(0, 0, 0, True, True)
            batch(1, 0, 1, False, True)
            dve.wait_ge(mlp_loaded, 16 * MLP_LOADS)
            for par in range(2):
                batch(2 + par, 1, par, False, False)
            with dve.Fori(2, TURNS) as turn:
                for par in range(2):
                    batch(2 * turn + par, turn, par, False, False)
            keep(NB - 2, TURNS - 1, 0, False)
            for layer in (1, 2):
                for piece in range(PIECES):
                    outer_piece(NB - 1, 1, layer, piece, False)
            keep(NB - 1, TURNS - 1, 1, False)

        @block.tensor
        def _(pe):
            pe.wait_ge(setup_loaded, 16 * SETUP_LOADS)

            def transposes(b, turn, par, q, first):
                half, f0 = q % 2, (q // 2) * TF
                if q % 2 == 0:
                    pe.wait_ge(gathered[par][q // 2], GATHER * (turn + 1))
                if first and q == 3:
                    pe.wait_ge(xpose_moved, 1)
                elif not first:
                    pe.wait_ge(xpose_moved, 2 * (TQ * b + q) - TQ)
                for i in range(TF):
                    mm = pe.transpose((first_ps(q) if first else t_ps)[:, i, :], x_rows[:, par, f0 + i, half * P:(half + 1) * P], ident[:, :])
                mm.then_inc(xpose_ready, 1)

            def form_yt(b, par, first):
                if not first:
                    pe.wait_ge(z0_moved, b)
                for half in range(HALVES):
                    for j in range(GROUPS):
                        mm = pe.matmul(turn_ps[j * GR:(j + 1) * GR, :], w12_sb[:, half, :],
                                       xt[:, par, half, j * GROUPS:(j + 1) * GROUPS, :],
                                       start=(half == 0), stop=(half == HALVES - 1))
                mm.then_inc(yt_ready, 1)

            def form_y(b):
                pe.wait_ge(yt_moved, b + 1)
                for i in range(NF // GROUPS):
                    mm = pe.transpose(turn_ps[:, i * P:(i + 1) * P], yt_sb[:, i * P:(i + 1) * P], ident[:, :])
                mm.then_inc(y_ready, 1)

            def form_z0(b, outputs):
                if outputs is not None:
                    pe.wait_ge(out_copied, outputs)
                pe.wait_ge(zs_moved, b + 1)
                pe.wait_ge(y_moved, b + 1)
                for i in range(BANK // P):
                    mm = pe.matmul(turn_ps[:, 0:NF], zs_sb[:, i * P:(i + 1) * P], sel[:, 0, 0:NF],
                                   start=(i == 0), stop=(i == BANK // P - 1))
                mm.then_inc(z0_ready, 1)

            def contract(b, par, k, first):
                ring = (NGRP * par + k // 2) % 2
                if k % 2 == 0 and not (first and k < 4):
                    pe.wait_ge(relu_done, NGRP * b + k // 2 - 1)
                if k == 0:
                    pe.wait_ge(xpose_moved, TQ * (2 * b + 1))
                    if first:
                        pe.wait_ge(first_squared, TQ)
                elif k <= DVE_SETS:
                    pe.wait_ge(dve_prod, NDVE * b + min(2 * k, NDVE))
                if k == DVE_SETS:
                    pe.wait_ge(pool_prod, NPOOL * (b + 1))
                src = (sq[:, :, :, :] if k == 0 else prod7[:, :, :, :] if k == 7 else
                       prod8[:, :, :, :] if k == 8 else prod[:, (k - 1) % PROD_RING, :, :, :])
                pairs = (NF // 2 if k == 8 else NF) // GROUPS
                col = (k % 2) * BANK
                for half in range(HALVES):
                    for j in range(GROUPS):
                        mm = pe.matmul(z_ps[j * GR:(j + 1) * GR, ring, col:col + pairs * P], w0_sb[:, half, :],
                                       src[:, half, j * pairs:(j + 1) * pairs, :],
                                       start=(half == 0), stop=(half == HALVES - 1))
                mm.then_inc(set_done, 1)

            def sum_pairs(b, par, g, first):
                ring = (NGRP * par + g) % 2
                pe.wait_ge(relu_done, NGRP * b + g + 1)
                if g == 0 and not first:
                    pe.wait_ge(zs_moved, b)
                for k in range(2 * g, min(2 * g + 2, NSETS)):
                    n = BANK if k < NSETS - 1 else BANK // 2
                    j = k % GROUPS
                    mm = pe.matmul(zs_ps[j * GR:(j + 1) * GR, 0:n],
                                   sel[:, 0 if k == 0 else 1, :],
                                   relu0[:, ring, (k % 2) * BANK:(k % 2) * BANK + n],
                                   start=(k < GROUPS), stop=(k + GROUPS >= NSETS), skip_group_check=True)
                mm.then_inc(pairs_summed, 1)

            def mlp_input(t, y_moves):
                pe.wait_ge(z_stored, 4 * (t + 1))
                pe.wait_ge(y_moved, y_moves)
                for i in range(2):
                    mm = pe.transpose(turn_ps[:, i * P:(i + 1) * P], cat[:, i, :], ident[:, :])
                mm.then_inc(feat_ps_ready, 1)

            def mlp_pair(t, i, moved=None):
                if i == 0:
                    pe.wait_ge(xpose_moved, moved)
                    pe.wait_ge(feat_ready, t + 1)
                elif 2 * i == M1:
                    pe.wait_ge(h_done, MB * t + M1)
                for m in (2 * i, 2 * i + 1):
                    if m < M1:
                        mm = pe.matmul(mlp_ps(m), w1_sb[:, m * P:(m + 1) * P], feat[:, :], start=True, stop=True)
                    else:
                        for k in range(M1):
                            mm = pe.matmul(mlp_ps(m), w2_sb[:, k, (m - M1) * P:(m - M1 + 1) * P], h1[:, k, :],
                                           start=(k == 0), stop=(k == M1 - 1))
                mm.then_inc(h_ready, 1)

            def mlp_output(t):
                pe.wait_ge(h_done, MB * (t + 1))
                for k in range(M2):
                    mm = pe.matmul(turn_ps[0:1, 0:MC], w3_sb[:, k:k + 1], h2[:, k, :],
                                   start=(k == 0), stop=(k == M2 - 1))
                mm.then_inc(out_ready, 1)

            def batch(b, turn, par, first, last, mlp=None):
                for k in range(NSETS):
                    if k in (2, 4, 6):
                        sum_pairs(b, par, k // 2 - 1, first)
                    if mlp is not None and k == 6:
                        mlp_pair(mlp, 0, TQ * (2 * (b if last else b + 1) + 1))
                        mlp_pair(mlp, 1)
                    contract(b, par, k, first)
                    if mlp is not None and k == 7:
                        mlp_pair(mlp, 2)
                    if k == 0 and not first:
                        sum_pairs(b - 1, 1 - par, NGRP - 1, False)
                    if k in XPOSE_AT and not last:
                        transposes(b + 1, turn + par, 1 - par, XPOSE_AT.index(k), False)
                    if k == 1 and not first:
                        form_z0(b - 1, turn - 1 if par == 0 and not (isinstance(turn, int) and turn < 2) else None)
                    if k == 3:
                        form_yt(b, par, first)
                    if k == 4:
                        form_y(b)
                    if mlp is not None and k == 5:
                        mlp_input(mlp, b + 1)
                sum_pairs(b, par, NGRP - 2, first)
                if mlp is not None:
                    mlp_output(mlp)

            for q in range(TQ):
                transposes(0, 0, 0, q, True)
            batch(0, 0, 0, True, False)
            batch(1, 0, 1, False, False)
            pe.wait_ge(mlp_loaded, 16 * MLP_LOADS)
            pe.wait_ge(zeroed, 3)
            batch(2, 1, 0, False, False)
            batch(3, 1, 1, False, False, mlp=0)
            with pe.Fori(2, TURNS - 1) as turn:
                batch(2 * turn, turn, 0, False, False)
                batch(2 * turn + 1, turn, 1, False, False, mlp=turn - 1)
            batch(NB - 2, TURNS - 1, 0, False, False)
            batch(NB - 1, TURNS - 1, 1, False, True, mlp=TURNS - 2)
            sum_pairs(NB - 1, 1, NGRP - 1, False)
            form_z0(NB - 1, TURNS - 1)
            mlp_input(TURNS - 1, NB)
            for i in range(MB // 2):
                mlp_pair(TURNS - 1, i, TQ * (2 * NB - 1))
            mlp_output(TURNS - 1)


def kernel(**inputs):
    import concourse.bacc as bacc
    from concourse.bass_utils import run_bass_kernel_spmd as run

    a = {k: np.asarray(v) for k, v in inputs.items()}
    n = a["ids"].shape[0]
    nb = n // P
    ws = a["L0_rec_Ws"]
    bs = a["L0_rec_bs"]
    sel = np.zeros((GROUPS, GR, 2, GR), np.float32)
    for o in range(NF):
        sel[:, o, 0, o] = 1.0
        sel[:, o, 1, o] = 2.0
    arrays = {f"tbl_{f}": a[f"tbl_{f}"] for f in range(NF)}
    arrays |= {
        "ids": a["ids"].reshape(nb, P, NF).transpose(1, 0, 2).reshape(P, nb * NF),
        "w0t": ws[0].T,
        "w12t": ws[1:].reshape(2 * NF, E).T,
        "bias0": bs[0].reshape(NF, 1),
        "bias12": bs[1:].reshape(1, 2 * NF),
        "dense": a["dense_ctx"].reshape(nb, P, -1).transpose(1, 0, 2),
        "w1": a["W_top1"],
        "b1": a["b_top1"].reshape(-1, P).T,
        "w2": a["W_top2"],
        "b2": a["b_top2"].reshape(-1, P).T,
        "w3": a["W_top3"].reshape(-1, P).T,
        "identity": np.eye(P, dtype=np.float32),
        "sel_out": sel.reshape(P, 2, GR),
    }
    arrays = {k: np.ascontiguousarray(v) for k, v in arrays.items()}
    nc = bacc.Bacc("TRN2", target_bir_lowering=False, num_devices=1)
    args = [nc.dram_tensor(f"in_{k}", v.shape, mybir.dt.from_np(v.dtype), kind="ExternalInput").ap()
            for k, v in arrays.items()]
    out = nc.dram_tensor("out_y", (1, n), F32, kind="ExternalOutput").ap()
    build(nc, args[:NF], *args[NF:], out)
    r = run(nc, [{f"in_{k}": v for k, v in arrays.items()}], core_ids=[0])
    return r.results[0]["out_y"].reshape(n, 1)
```

```python
from contextlib import ExitStack

import numpy as np
import concourse.bass as bass
from concourse import mybir

F32 = mybir.dt.float32
BF16 = mybir.dt.bfloat16
I32 = mybir.dt.int32
U32 = mybir.dt.uint32
ALU = mybir.AluOpType
ACT = mybir.ActivationFunctionType

P = 128
NF = 16
E = 256
HALVES = E // P
NL = 3
GROUPS = 4
GR = P // GROUPS
NSETS = NF // 2 + 1
SET = NF * P
DVE_SETS = 6
DVE_ORDER = (1, 2, 3, 6, 4, 5)
DVE_COUNTS = (2, 4, 6, 7, 9, 11)
NDVE = DVE_COUNTS[-1]
NPOOL = 4
PEELED = 6
PROD_RING = 3
ORDER = (0, 7, 1, 8, 2, 3, 6, 4, 5)
FIRST_ORDER = (0, 1, 2, 3, 7, 8, 6, 4, 5)
ADDER = (0, 1, 2, 0, 3, 1, 2, 3, 0)
NGRP = (NSETS + 1) // 2
BANK = 512
TQ = 4
XPOSE_AT = (0, 1, 4, 5)
TF = NF * HALVES // TQ
PIECES = 2
PO = NF // PIECES
NTT = 2 * PIECES
NACC = 2 * NF
JUNK = 4


def build(nc, tables, ids, w0t, w12t, bias0, bias12, dense, w1, b1, w2, b2, w3,
          identity, sel_out, y_out):
    NB = ids.shape[1] // NF
    TURNS = NB // 2
    H1, H2 = w1.shape[1], w2.shape[1]
    M1, M2 = H1 // P, H2 // P
    MB = M1 + M2
    ND = dense.shape[2]
    KH = NL * NF + ND
    MC = 2 * P

    with ExitStack() as ctx:
        def sb(name, shape, dt=F32):
            return ctx.enter_context(nc.sbuf_tensor(name, shape, dt))

        def ps(name, shape):
            return ctx.enter_context(nc.psum_tensor(name, shape, F32))

        def sem(name):
            return ctx.enter_context(nc.semaphore(name))

        x_rows = sb("x_rows", [P, 2, NF, E])
        xt = sb("xt", [P, 2, HALVES, NF, P])
        sq = sb("sq", [P, HALVES, NF, P])
        prod = sb("prod", [P, PROD_RING, HALVES, NF, P])
        prod7 = sb("prod7", [P, HALVES, NF, P])
        prod8 = sb("prod8", [P, HALVES, NF // 2, P])
        relu0 = sb("relu0", [P, 2, 2 * BANK])
        zs_sb = sb("zs_sb", [P, BANK])
        yt_sb = sb("yt_sb", [P, BANK])
        y_sb = sb("y_sb", [P, 2, 2, NF, NF])
        outer = sb("outer", [P, PIECES, PO, NF, NF])
        junk = sb("junk", [P, JUNK, NF * NF], BF16)
        zeros = sb("zeros", [P, NF * NF])
        z_cur = sb("z_cur", [P, 2, NL, NF])
        dense_sb = sb("dense_sb", [P, NB, ND])
        cat = sb("cat", [P, 2, P])
        feat = sb("feat", [KH, MC])
        h1 = sb("h1", [P, M1, MC])
        h2 = sb("h2", [P, M2, MC])
        y_row = sb("y_row", [1, MC])
        ids_sb = sb("ids_sb", [P, NB * NF], I32)
        ids_cur = sb("ids_cur", [P, 2, NF], U32)
        w0_sb = sb("w0_sb", [P, HALVES, GR])
        w12_sb = sb("w12_sb", [P, HALVES, 2 * NF])
        bias0_sb = sb("bias0_sb", [P, 1])
        bias12_sb = sb("bias12_sb", [P, 2, NF])
        ident = sb("ident", [P, P])
        sel = sb("sel", [P, 2, GR])
        w1_sb = sb("w1_sb", [KH, H1])
        b1_sb = sb("b1_sb", [P, M1])
        w2_sb = sb("w2_sb", [P, M1, H2])
        b2_sb = sb("b2_sb", [P, M2])
        w3_sb = sb("w3_sb", [P, M2])

        z_ps = ps("z_ps", [P, 2, 2 * BANK])
        t_ps = ps("t_ps", [P, TF, P])
        zs_ps = ps("zs_ps", [P, BANK])
        turn_ps = ps("turn_ps", [P, BANK])

        setup_loaded = sem("setup_loaded")
        zeroed = sem("zeroed")
        ids_loaded = sem("ids_loaded")
        mlp_loaded = sem("mlp_loaded")
        ids_copied = sem("ids_copied")
        gathered = [[sem(f"gathered{par}{half}") for half in range(2)] for par in range(2)]
        batches_free = sem("batches_free")
        xpose_ready = sem("xpose_ready")
        xpose_moved = sem("xpose_moved")
        first_squared = sem("first_squared")
        dve_prod = sem("dve_prod")
        first_prod = sem("first_prod")
        pool_prod = sem("pool_prod")
        set_done = sem("set_done")
        relu_done = sem("relu_done")
        pairs_summed = sem("pairs_summed")
        zs_moved = sem("zs_moved")
        z0_ready = sem("z0_ready")
        z0_moved = sem("z0_moved")
        yt_ready = sem("yt_ready")
        yt_moved = sem("yt_moved")
        y_ready = sem("y_ready")
        y_moved = sem("y_moved")
        outer_done = sem("outer_done")
        acc_done = sem("acc_done")
        dve_acc = sem("dve_acc")
        z_stored = sem("z_stored")
        feat_ps_ready = sem("feat_ps_ready")
        feat_ready = sem("feat_ready")
        h_ready = sem("h_ready")
        h_done = sem("h_done")
        out_ready = sem("out_ready")
        out_copied = sem("out_copied")
        stored = sem("stored")

        SETUP_LOADS = 5 + GROUPS
        MLP_LOADS = 6
        GATHER = 16 * NF // 2

        block = ctx.enter_context(nc.Block())

        def mlp_ps(m):
            if m < M1:
                return t_ps[:, 2 * m:2 * m + 2, :].rearrange("p i s -> p (i s)")
            return turn_ps[:, (m - M1) * MC:(m - M1 + 1) * MC]

        def first_ps(q):
            return t_ps[:, :, :] if q in (0, 3) else z_ps[:, q - 1, :].rearrange("p (f s) -> p f s", f=TF)

        def acc_tail(nb, pieces):
            return NACC * (nb - 3) + NF + PO * pieces

        def late(b):
            return max(0, b - (NB - 3)) if isinstance(b, int) else 0

        def dve_made(b, d):
            i = DVE_ORDER.index(d)
            missing = max(0, late(b) - 1) + (late(b) > 0 and i > DVE_ORDER.index(DVE_SETS))
            return NDVE * b + DVE_COUNTS[i] - missing

        def pool_made(b, product):
            return NPOOL * (b - 1) + max(0, late(b) - 1) + product

        def buffer(d):
            return DVE_ORDER.index(d) % PROD_RING

        def buffer_free(b, d, first=False):
            i = DVE_ORDER.index(d)
            if i >= PROD_RING:
                return done_sets(b, DVE_ORDER[i - PROD_RING])
            return None if first else done_sets(b - 1, DVE_ORDER[i + DVE_SETS - PROD_RING])

        def order(b):
            return FIRST_ORDER if isinstance(b, int) and b == 0 else ORDER

        def done_sets(b, d):
            return NSETS * b + order(b).index(d) + 1

        def columns(b, step):
            return BANK // 2 if order(b)[step] == NF // 2 else BANK

        @block.sync
        def _(sp):
            sp.dma_start(ids_sb[:, :], ids).then_inc(ids_loaded, 16)
            sp.dma_start(ident[:, :], identity).then_inc(setup_loaded, 16)
            sp.dma_start(w12_sb[:, :, :], w12t.rearrange("(h p) o -> p h o", p=P)).then_inc(setup_loaded, 16)
            sp.dma_start(sel[:, :, :], sel_out).then_inc(setup_loaded, 16)
            sp.dma_start(bias12_sb[:, :, :].rearrange("p l o -> p (l o)"),
                         bias12.to_broadcast([P, 2 * NF])).then_inc(setup_loaded, 16)
            sp.wait_ge(zeroed, 2)
            sp.dma_start(w0_sb[:, :, 0:NF], w0t.rearrange("(h p) o -> p h o", p=P)).then_inc(setup_loaded, 16)
            for j in range(GROUPS):
                sp.dma_start(bias0_sb[j * GR:j * GR + NF, :], bias0).then_inc(setup_loaded, 16)
            sp.dma_start(dense_sb[:, :, :], dense).then_inc(mlp_loaded, 16)
            sp.dma_start(w1_sb[:, :], w1).then_inc(mlp_loaded, 16)
            sp.dma_start(b1_sb[:, :], b1).then_inc(mlp_loaded, 16)
            sp.dma_start(w2_sb[:, :, :], w2.rearrange("(m p) n -> p m n", p=P)).then_inc(mlp_loaded, 16)
            sp.dma_start(b2_sb[:, :], b2).then_inc(mlp_loaded, 16)
            sp.dma_start(w3_sb[:, :], w3).then_inc(mlp_loaded, 16)
            with sp.Fori(0, TURNS) as turn:
                sp.wait_ge(out_copied, turn + 1)
                sp.dma_start(y_out[:, bass.ds(MC * turn, MC)], y_row[:, :]).then_inc(stored, 16)
            sp.wait_ge(stored, 16 * TURNS)

        @block.gpsimd
        def _(pool):
            def products_wrap(b, par):
                d = DVE_SETS
                pool.wait_ge(set_done, buffer_free(b, d))
                pool.tensor_tensor(prod[:, buffer(d), :, NF - d:NF, :], xt[:, par, :, NF - d:NF, :],
                                   xt[:, par, :, 0:d, :], ALU.mult).then_inc(pool_prod, 1)

            def gather(b, turn, par, half, first=False):
                if half == 0:
                    if not first:
                        pool.wait_ge(gathered[par][0], GATHER * turn)
                        pool.wait_ge(gathered[par][1], GATHER * turn)
                    pool.tensor_copy(ids_cur[:, par, :], ids_sb[:, bass.ds(NF * b, NF)]).then_inc(ids_copied, 1)
                    pool.wait_ge(ids_copied, b + 1)
                if not first:
                    pool.wait_ge(xpose_ready, TQ * (b - 2) + 2 * (half + 1))
                pool.sem_inc(batches_free, 1)
                for f in range(half * NF // 2, (half + 1) * NF // 2):
                    pool.indirect_dma_start(
                        out=x_rows[:, par, f, :], out_offset=None, in_=tables[f],
                        in_offset=bass.IndirectOffsetOnAxis(ap=ids_cur[:, par, f:f + 1], axis=0),
                    ).then_inc(gathered[par][half], 16)

            def products(b, par):
                pool.wait_ge(xpose_moved, TQ * (2 * b + 1))
                pool.wait_ge(set_done, done_sets(b - 1, 7))
                d = 7
                pool.tensor_tensor(prod7[:, :, 0:NF - d, :], xt[:, par, :, 0:NF - d, :],
                                   xt[:, par, :, d:NF, :], ALU.mult).then_inc(pool_prod, 1)
                pool.tensor_tensor(prod7[:, :, NF - d:NF, :], xt[:, par, :, NF - d:NF, :],
                                   xt[:, par, :, 0:d, :], ALU.mult).then_inc(pool_prod, 1)
                pool.wait_ge(set_done, done_sets(b - 1, 8))
                d = NF // 2
                pool.tensor_tensor(prod8[:, :, :, :], xt[:, par, :, 0:d, :],
                                   xt[:, par, :, d:NF, :], ALU.mult).then_inc(pool_prod, 1)

            pool.wait_ge(ids_loaded, 16)
            for b in range(2):
                for half in range(2):
                    gather(b, 0, b, half, first=True)
            gather(2, 1, 0, 0)

            def batch(b, turn, par, ahead=2):
                products(b, par)
                if ahead > 0:
                    gather(b + 1, turn + par, 1 - par, 1)
                products_wrap(b, par)
                if late(b) > 0:
                    d = DVE_SETS
                    pool.tensor_tensor(prod[:, buffer(d), :, 0:NF - d, :], xt[:, par, :, 0:NF - d, :],
                                       xt[:, par, :, d:NF, :], ALU.mult).then_inc(pool_prod, 1)
                if late(b) == 2:
                    d = 5
                    pool.wait_ge(set_done, buffer_free(b, d))
                    pool.tensor_tensor(prod[:, buffer(d), :, 0:NF - d, :], xt[:, par, :, 0:NF - d, :],
                                       xt[:, par, :, d:NF, :], ALU.mult).then_inc(pool_prod, 1)
                if ahead > 1:
                    gather(b + 2, turn + 1, par, 0)

            batch(1, 0, 1)
            with pool.Fori(1, TURNS - 1) as turn:
                for par in range(2):
                    batch(2 * turn + par, turn, par)
            for par in range(2):
                batch(NB - 2 + par, TURNS - 1, par, ahead=1 - par)

        @block.scalar
        def _(act):
            act.wait_ge(setup_loaded, 16 * SETUP_LOADS)

            def move_xt(b, par, q, first):
                half, f0 = q % 2, (q // 2) * TF
                act.wait_ge(xpose_ready, TQ * b + q + 1)
                if not first and q == 0:
                    act.wait_ge(dve_prod, NDVE * (b - 1))
                    if isinstance(b, int) and b == 2:
                        act.wait_ge(first_prod, 2)
                    else:
                        act.wait_ge(pool_prod, NPOOL * (b - 2))
                    act.wait_ge(y_ready, b - 1)
                act.activation(xt[:, par, half, f0:f0 + TF, :], t_ps[:, :, :], ACT.Copy).then_inc(xpose_moved, 1)
                if q == 0:
                    act.wait_ge(set_done, done_sets(b - 1, 0))
                act.activation(sq[:, half, f0:f0 + TF, :], t_ps[:, :, :], ACT.Square).then_inc(xpose_moved, 1)

            def relu_group(b, par, g, early):
                act.wait_ge(set_done, NSETS * b + min(2 * g + 2, NSETS))
                if not early:
                    act.wait_ge(pairs_summed, NGRP * b + g - 1)
                ring = (NGRP * par + g) % 2
                n = BANK + columns(b, 2 * g + 1) if 2 * g + 1 < NSETS else columns(b, 2 * g)
                act.activation(relu0[:, ring, 0:n], z_ps[:, ring, 0:n], ACT.Relu,
                               bias=bias0_sb[:, :]).then_inc(relu_done, 1)

            def move_zs(b):
                act.wait_ge(pairs_summed, NGRP * (b + 1))
                act.activation(zs_sb[:, :], zs_ps[:, :], ACT.Copy).then_inc(zs_moved, 1)

            def move_yt(b):
                act.wait_ge(yt_ready, b + 1)
                act.activation(yt_sb[:, :], turn_ps[:, :], ACT.Copy).then_inc(yt_moved, 1)

            def move_y(b, par, first):
                act.wait_ge(y_ready, b + 1)
                if not first:
                    act.wait_ge(outer_done, NTT * (b - 1))
                act.activation(y_sb[:, par, :, :, :].rearrange("p l o (j i) -> p (l o) j i", j=GROUPS),
                               turn_ps[:, :].rearrange("p (i j c) -> p c j i", i=NF // GROUPS, j=GROUPS),
                               ACT.Copy).then_inc(y_moved, 1)

            def sum_piece(b, par, layer, piece, early, tail=None):
                act.wait_ge(outer_done, NTT * b + PIECES * (layer - 1) + piece + 1)
                done = NACC * b + NF * (layer - 1) + PO * piece if tail is None else acc_tail(NB, tail)
                for i in range(PO):
                    o = PO * piece + i
                    if not (early and layer == 1 and o < JUNK):
                        act.wait_ge(acc_done, done + i - JUNK + 1)
                    act.activation(junk[:, i % JUNK, :], outer[:, piece, i, :, :].rearrange("p f g -> p (f g)"),
                                   ACT.Relu, bias=bias12_sb[:, layer - 1, o:o + 1],
                                   accum_out=z_cur[:, par, layer, o:o + 1]).then_inc(acc_done, 1)

            def mlp_input(t):
                act.wait_ge(feat_ps_ready, t + 1)
                act.activation(feat[:, :], turn_ps[0:KH, 0:MC], ACT.Copy).then_inc(feat_ready, 1)

            def mlp_relu(t, m):
                if m % 2 == 0:
                    act.wait_ge(h_ready, MB // 2 * t + m // 2 + 1)
                src = mlp_ps(m)
                if m < M1:
                    act.activation(h1[:, m, :], src, ACT.Relu, bias=b1_sb[:, m:m + 1]).then_inc(h_done, 1)
                else:
                    act.activation(h2[:, m - M1, :], src, ACT.Relu,
                                   bias=b2_sb[:, m - M1:m - M1 + 1]).then_inc(h_done, 1)

            def mlp_output(t, first):
                act.wait_ge(out_ready, t + 1)
                if not first:
                    act.wait_ge(stored, 16 * t)
                act.activation(y_row[:, :], turn_ps[0:1, 0:MC], ACT.Copy).then_inc(out_copied, 1)

            def mlp_layer(t, layer):
                for m in (range(M1) if layer == 0 else range(M1, MB)):
                    mlp_relu(t, m)

            def batch(b, turn, par, age, last=False):
                first = age == 0
                mlp = turn - 2 if age > 3 else None
                if age > 0:
                    move_zs(b - 1)
                if mlp is not None and par == 0:
                    mlp_input(mlp)
                if not last:
                    move_xt(b + 1, 1 - par, 0, first)
                relu_group(b, par, 0, first)
                if age > 1:
                    sum_piece(b - 2, par, 2, 0, False, tail=0 if last else None)
                if not last:
                    move_xt(b + 1, 1 - par, 1, first)
                relu_group(b, par, 1, first)
                if age > 1 and not last:
                    sum_piece(b - 2, par, 2, 1, False)
                if not last:
                    move_xt(b + 1, 1 - par, 2, first)
                relu_group(b, par, 2, False)
                if not last:
                    move_xt(b + 1, 1 - par, 3, first)
                move_yt(b)
                if age > 0:
                    sum_piece(b - 1, 1 - par, 1, 0, age == 1, tail=1 if last else None)
                move_y(b, par, age < 2)
                if age > 0 and not last:
                    sum_piece(b - 1, 1 - par, 1, 1, age == 1)
                relu_group(b, par, 3, False)
                if mlp is not None:
                    mlp_layer(mlp, par)
                relu_group(b, par, 4, False)
                if mlp is not None and par == 1:
                    mlp_output(mlp, age == 5)

            for half in range(HALVES):
                f0 = half * TF
                for q in (2 * half, 2 * half + 1):
                    act.wait_ge(xpose_ready, q + 1)
                    act.activation(xt[:, 0, q % 2, f0:f0 + TF, :], first_ps(q), ACT.Copy).then_inc(xpose_moved, 1)
                for q in (2 * half, 2 * half + 1):
                    act.wait_ge(xpose_moved, q + 1)
                    act.activation(sq[:, q % 2, f0:f0 + TF, :], xt[:, 0, q % 2, f0:f0 + TF, :],
                                   ACT.Square).then_inc(first_squared, 1)
            for b in range(PEELED):
                if b == 4:
                    act.wait_ge(mlp_loaded, 16 * MLP_LOADS)
                batch(b, b // 2, b % 2, b)
            with act.Fori(PEELED // 2, TURNS - 1) as turn:
                for par in range(2):
                    batch(2 * turn + par, turn, par, PEELED)
            batch(NB - 2, TURNS - 1, 0, PEELED)
            batch(NB - 1, TURNS - 1, 1, PEELED, last=True)
            move_zs(NB - 1)
            sum_piece(NB - 2, 0, 2, 0, False, tail=2)
            mlp_input(TURNS - 2)
            sum_piece(NB - 1, 1, 1, 0, False, tail=3)
            mlp_layer(TURNS - 2, 0)
            sum_piece(NB - 1, 1, 2, 0, False, tail=4)
            mlp_layer(TURNS - 2, 1)
            mlp_output(TURNS - 2, False)
            mlp_input(TURNS - 1)
            for layer in range(2):
                mlp_layer(TURNS - 1, layer)
            mlp_output(TURNS - 1, False)

        @block.vector
        def _(dve):
            dve.memset(w0_sb[:, :, :], 0.0).then_inc(zeroed, 1)
            dve.memset(bias0_sb[:, :], 0.0).then_inc(zeroed, 1)
            dve.memset(cat[:, :, KH:P], 0.0).then_inc(zeroed, 1)
            dve.memset(zeros[:, :], 0.0).then_inc(zeroed, 1)

            def products(b, par, d, first):
                ring = buffer(d)
                if d == 1:
                    dve.wait_ge(xpose_moved, TQ * (2 * b + 1))
                free = buffer_free(b, d, first)
                if free is not None:
                    dve.wait_ge(set_done, free)
                f0 = TF - d if first and d <= PROD_RING else 0
                wrapped = d < DVE_SETS or first
                mm = dve.tensor_tensor(prod[:, ring, :, f0:NF - d, :], xt[:, par, :, f0:NF - d, :],
                                       xt[:, par, :, f0 + d:NF, :], ALU.mult)
                if not (first and d == DVE_SETS):
                    mm.then_inc(dve_prod, 1)
                if wrapped:
                    dve.tensor_tensor(prod[:, ring, :, NF - d:NF, :], xt[:, par, :, NF - d:NF, :],
                                      xt[:, par, :, 0:d, :], ALU.mult).then_inc(dve_prod, 1)

            def move_z0(b, par):
                dve.wait_ge(z0_ready, b + 1)
                dve.tensor_copy(z_cur[:, par, 0, :], turn_ps[:, 0:NF]).then_inc(z0_moved, 1)

            def outer_piece(b, par, layer, piece, early, tail=None):
                if layer == 1 and piece == 0:
                    dve.wait_ge(z0_moved, b + 1)
                    dve.wait_ge(y_moved, b + 1)
                if tail is None:
                    if layer == 2 and piece == 0:
                        dve.wait_ge(acc_done, NACC * b + NF)
                    if not (early and layer == 1):
                        dve.wait_ge(acc_done, NACC * b + NF * (layer - 1) + PO * (piece - 1))
                elif tail == 0:
                    dve.wait_ge(acc_done, acc_tail(NB, 0))
                else:
                    dve.wait_ge(acc_done, acc_tail(NB, tail))
                    dve.wait_ge(dve_acc, PO * tail)
                z = z_cur[:, par, layer - 1, :]
                y = y_sb[:, par, layer - 1, piece * PO:(piece + 1) * PO, :].rearrange("p o f -> p (o f)")
                dve.tensor_tensor(outer[:, piece, :, :, :].rearrange("p o f g -> p (o f) g"),
                                  y.unsqueeze(2).to_broadcast([P, PO * NF, NF]),
                                  z.unsqueeze(1).to_broadcast([P, PO * NF, NF]), ALU.mult).then_inc(outer_done, 1)

            def sum_piece(b, par, layer, piece):
                dve.wait_ge(outer_done, NTT * b + PIECES * (layer - 1) + piece + 1)
                for i in range(PO):
                    o = PO * piece + i
                    relu = outer[:, piece, i, :, :].rearrange("p f g -> p (f g)")
                    dve.scalar_tensor_tensor(relu, relu, bias12_sb[:, layer - 1, o:o + 1], zeros[:, :],
                                             ALU.add, ALU.max, accum_out=z_cur[:, par, layer, o:o + 1]
                                             ).then_inc(dve_acc, 1)

            def keep(b, turn, par, early, tail=None):
                if tail is None:
                    dve.wait_ge(acc_done, NACC * (b + 1))
                else:
                    dve.wait_ge(acc_done, acc_tail(NB, tail))
                    dve.wait_ge(dve_acc, PO * tail)
                if not early:
                    dve.wait_ge(feat_ps_ready, turn)
                dve.tensor_copy(cat[:, par, 0:NL * NF],
                                z_cur[:, par, :, :].rearrange("p l o -> p (l o)")).then_inc(z_stored, 1)
                dve.tensor_copy(cat[:, par, NL * NF:KH].unsqueeze(1), dense_sb[:, bass.ds(b, 1), :]
                                ).then_inc(z_stored, 1)

            def batch(b, turn, par, age, last=False):
                products(b, par, 1, age == 0)
                if age > 1:
                    outer_piece(b - 2, par, 2, 0, False, tail=0 if last else None)
                products(b, par, 2, age == 0)
                if age > 1:
                    outer_piece(b - 2, par, 2, 1, False, tail=0 if last else None)
                if last:
                    sum_piece(b - 2, par, 2, 1)
                products(b, par, 3, age == 0)
                if age == 0:
                    d = DVE_SETS + 1
                    dve.tensor_tensor(prod7[:, :, 0:NF - d, :], xt[:, 0, :, 0:NF - d, :],
                                      xt[:, 0, :, d:NF, :], ALU.mult)
                    dve.tensor_tensor(prod7[:, :, NF - d:NF, :], xt[:, 0, :, NF - d:NF, :],
                                      xt[:, 0, :, 0:d, :], ALU.mult).then_inc(first_prod, 1)
                    d = NF // 2
                    dve.tensor_tensor(prod8[:, :, :, :], xt[:, 0, :, 0:d, :],
                                      xt[:, 0, :, d:NF, :], ALU.mult).then_inc(first_prod, 1)
                if age > 0:
                    move_z0(b - 1, 1 - par)
                if not late(b):
                    products(b, par, 6, age == 0)
                if age > 0:
                    outer_piece(b - 1, 1 - par, 1, 0, age == 1, tail=1 if last else None)
                products(b, par, 4, age == 0)
                if age > 0:
                    outer_piece(b - 1, 1 - par, 1, 1, age == 1, tail=1 if last else None)
                if last:
                    dve.wait_ge(set_done, buffer_free(b, 5))
                    dve.tensor_tensor(prod[:, buffer(5), :, NF - 5:NF, :], xt[:, par, :, NF - 5:NF, :],
                                      xt[:, par, :, 0:5, :], ALU.mult).then_inc(dve_prod, 1)
                    sum_piece(b - 1, 1 - par, 1, 1)
                if age > 1:
                    keep(b - 2, turn - 1, par, age < 4, tail=1 if last else None)
                if late(b) < 2:
                    products(b, par, 5, age == 0)

            dve.wait_ge(xpose_moved, 2)
            for d in range(1, PROD_RING + 1):
                dve.tensor_tensor(prod[:, buffer(d), :, 0:TF - d, :], xt[:, 0, :, 0:TF - d, :],
                                  xt[:, 0, :, d:TF, :], ALU.mult)
            for b in range(PEELED):
                if b == 2:
                    dve.wait_ge(mlp_loaded, 16 * MLP_LOADS)
                batch(b, b // 2, b % 2, b)
            with dve.Fori(PEELED // 2, TURNS - 1) as turn:
                for par in range(2):
                    batch(2 * turn + par, turn, par, PEELED)
            batch(NB - 2, TURNS - 1, 0, PEELED)
            batch(NB - 1, TURNS - 1, 1, PEELED, last=True)
            tail = 2
            for b, layer in ((NB - 2, 2), (NB - 1, 1), (NB - 1, 2)):
                if layer == 1:
                    move_z0(b, b % 2)
                outer_piece(b, b % 2, layer, 0, False, tail=tail)
                outer_piece(b, b % 2, layer, 1, False, tail=tail)
                sum_piece(b, b % 2, layer, 1)
                tail += 1
                if (b, layer) == (NB - 1, 1):
                    keep(NB - 2, TURNS - 1, 0, False, tail=3)
            keep(NB - 1, TURNS - 1, 1, False, tail=5)

        @block.tensor
        def _(pe):
            pe.wait_ge(setup_loaded, 16 * SETUP_LOADS)

            def transposes(b, turn, par, q, first, hidden=None):
                half, f0 = q % 2, (q // 2) * TF
                if q % 2 == 0:
                    pe.wait_ge(gathered[par][q // 2], GATHER * (turn + 1))
                if hidden is not None:
                    pe.wait_ge(h_done, hidden)
                if first and q == 3:
                    pe.wait_ge(xpose_moved, 1)
                elif not first:
                    pe.wait_ge(xpose_moved, 2 * (TQ * b + q) - TQ)
                for i in range(TF):
                    mm = pe.transpose((first_ps(q) if first else t_ps)[:, i, :], x_rows[:, par, f0 + i, half * P:(half + 1) * P], ident[:, :])
                mm.then_inc(xpose_ready, 1)

            def form_yt(b, par, first):
                if not first:
                    pe.wait_ge(z0_moved, b)
                for half in range(HALVES):
                    for j in range(GROUPS):
                        mm = pe.matmul(turn_ps[j * GR:(j + 1) * GR, :], w12_sb[:, half, :],
                                       xt[:, par, half, j * GROUPS:(j + 1) * GROUPS, :],
                                       start=(half == 0), stop=(half == HALVES - 1))
                mm.then_inc(yt_ready, 1)

            def form_y(b):
                pe.wait_ge(yt_moved, b + 1)
                for i in range(NF // GROUPS):
                    mm = pe.transpose(turn_ps[:, i * P:(i + 1) * P], yt_sb[:, i * P:(i + 1) * P], ident[:, :])
                mm.then_inc(y_ready, 1)

            def form_z0(b, mlp):
                if mlp is not None:
                    pe.wait_ge(feat_ready, mlp + 1)
                pe.wait_ge(zs_moved, b + 1)
                pe.wait_ge(y_moved, b + 1)
                for i in range(BANK // P):
                    mm = pe.matmul(turn_ps[:, 0:NF], zs_sb[:, i * P:(i + 1) * P], sel[:, 0, 0:NF],
                                   start=(i == 0), stop=(i == BANK // P - 1))
                mm.then_inc(z0_ready, 1)

            def contract(b, par, step, first):
                d = order(b)[step]
                ring = (NGRP * par + step // 2) % 2
                if step % 2 == 0 and not (first and step < 4):
                    pe.wait_ge(relu_done, NGRP * b + step // 2 - 1)
                if d == 0:
                    pe.wait_ge(xpose_moved, TQ * (2 * b + 1))
                    if first:
                        pe.wait_ge(first_squared, TQ)
                elif late(b) == 2 and d == 5:
                    pe.wait_ge(pool_prod, pool_made(b, NPOOL + 2))
                    pe.wait_ge(dve_prod, dve_made(b, 4) + 1)
                elif d < DVE_SETS or (d == DVE_SETS and not late(b)):
                    pe.wait_ge(dve_prod, dve_made(b, d))
                if first and d > DVE_SETS:
                    pe.wait_ge(first_prod, d - DVE_SETS)
                elif not first and d >= DVE_SETS:
                    pe.wait_ge(pool_prod, pool_made(b, {7: 2, 8: 3, DVE_SETS: NPOOL + (late(b) > 0)}[d]))
                src = (sq[:, :, :, :] if d == 0 else prod7[:, :, :, :] if d == 7 else
                       prod8[:, :, :, :] if d == 8 else prod[:, buffer(d), :, :, :])
                pairs = columns(b, step) // P
                col = (step % 2) * BANK
                for half in range(HALVES):
                    for j in range(GROUPS):
                        mm = pe.matmul(z_ps[j * GR:(j + 1) * GR, ring, col:col + pairs * P], w0_sb[:, half, :],
                                       src[:, half, j * pairs:(j + 1) * pairs, :],
                                       start=(half == 0), stop=(half == HALVES - 1))
                mm.then_inc(set_done, 1)

            def sum_pairs(b, par, g, first):
                ring = (NGRP * par + g) % 2
                pe.wait_ge(relu_done, NGRP * b + g + 1)
                if g == 0 and not first:
                    pe.wait_ge(zs_moved, b)
                for k in range(2 * g, min(2 * g + 2, NSETS)):
                    n = columns(b, k)
                    j = ADDER[k]
                    mm = pe.matmul(zs_ps[j * GR:(j + 1) * GR, 0:n],
                                   sel[:, 0 if order(b)[k] == 0 else 1, :],
                                   relu0[:, ring, (k % 2) * BANK:(k % 2) * BANK + n],
                                   start=(j not in ADDER[:k]), stop=(j not in ADDER[k + 1:]), skip_group_check=True)
                mm.then_inc(pairs_summed, 1)

            def mlp_input(t, y_moves):
                pe.wait_ge(z_stored, 4 * (t + 1))
                pe.wait_ge(y_moved, y_moves)
                if not (isinstance(t, int) and t == 0):
                    pe.wait_ge(out_copied, t)
                for i in range(2):
                    mm = pe.transpose(turn_ps[:, i * P:(i + 1) * P], cat[:, i, :], ident[:, :])
                mm.then_inc(feat_ps_ready, 1)

            def mlp_pair(t, i, moved=None):
                if moved is not None:
                    pe.wait_ge(xpose_moved, moved)
                if i == 0:
                    pe.wait_ge(feat_ready, t + 1)
                elif 2 * i == M1:
                    pe.wait_ge(h_done, MB * t + M1)
                for m in (2 * i, 2 * i + 1):
                    if m < M1:
                        mm = pe.matmul(mlp_ps(m), w1_sb[:, m * P:(m + 1) * P], feat[:, :], start=True, stop=True)
                    else:
                        for k in range(M1):
                            mm = pe.matmul(mlp_ps(m), w2_sb[:, k, (m - M1) * P:(m - M1 + 1) * P], h1[:, k, :],
                                           start=(k == 0), stop=(k == M1 - 1))
                mm.then_inc(h_ready, 1)

            def mlp_output(t):
                pe.wait_ge(h_done, MB * (t + 1))
                for k in range(M2):
                    mm = pe.matmul(turn_ps[0:1, 0:MC], w3_sb[:, k:k + 1], h2[:, k, :],
                                   start=(k == 0), stop=(k == M2 - 1))
                mm.then_inc(out_ready, 1)

            def batch(b, turn, par, age, last=False):
                first = age == 0
                mlp = turn - 2 if age > 3 else None
                for k in range(NSETS):
                    if k in (3, 5, 7):
                        sum_pairs(b, par, (k - 3) // 2, first)
                    if k == 0 and age > 0:
                        sum_pairs(b - 1, 1 - par, NGRP - 2, age == 1)
                    contract(b, par, k, first)
                    if k == 0 and age > 0:
                        sum_pairs(b - 1, 1 - par, NGRP - 1, False)
                    if mlp is not None and (k, par) == (0, 0):
                        mlp_input(mlp, b)
                    if k == 3 and age > 0:
                        form_z0(b - 1, mlp if par == 0 else None)
                    for q in range(TQ):
                        if XPOSE_AT[q] == k and not last:
                            hidden = MB * mlp + M1 if mlp is not None and par == 1 and q == 0 else None
                            transposes(b + 1, turn + par, 1 - par, q, False, hidden)
                    if k == 5:
                        form_yt(b, par, first)
                    if k == 6:
                        form_y(b)
                    if mlp is not None and (k, par) == (7, 0):
                        mlp_pair(mlp, 0, TQ * (2 * b + 3))
                        mlp_pair(mlp, 1)
                    if mlp is not None and (k, par) == (7, 1):
                        pe.wait_ge(y_moved, b + 1)
                        mlp_pair(mlp, M1 // 2)
                    if mlp is not None and (k, par) == (8, 1):
                        mlp_output(mlp)

            for q in range(TQ):
                transposes(0, 0, 0, q, True)
            for b in range(PEELED):
                if b == 4:
                    pe.wait_ge(mlp_loaded, 16 * MLP_LOADS)
                    pe.wait_ge(zeroed, 3)
                batch(b, b // 2, b % 2, b)
            with pe.Fori(PEELED // 2, TURNS - 1) as turn:
                for par in range(2):
                    batch(2 * turn + par, turn, par, PEELED)
            batch(NB - 2, TURNS - 1, 0, PEELED)
            batch(NB - 1, TURNS - 1, 1, PEELED, last=True)
            for g in (NGRP - 2, NGRP - 1):
                sum_pairs(NB - 1, 1, g, False)
            form_z0(NB - 1, None)
            pe.wait_ge(z0_moved, NB)
            for t in (TURNS - 2, TURNS - 1):
                mlp_input(t, NB)
                for i in range(MB // 2):
                    mlp_pair(t, i)
                mlp_output(t)


def kernel(**inputs):
    import concourse.bacc as bacc
    from concourse.bass_utils import run_bass_kernel_spmd as run

    a = {k: np.asarray(v) for k, v in inputs.items()}
    n = a["ids"].shape[0]
    nb = n // P
    ws = a["L0_rec_Ws"]
    bs = a["L0_rec_bs"]
    sel = np.zeros((GROUPS, GR, 2, GR), np.float32)
    for o in range(NF):
        sel[:, o, 0, o] = 1.0
        sel[:, o, 1, o] = 2.0
    arrays = {f"tbl_{f}": a[f"tbl_{f}"] for f in range(NF)}
    arrays |= {
        "ids": a["ids"].reshape(nb, P, NF).transpose(1, 0, 2).reshape(P, nb * NF),
        "w0t": ws[0].T,
        "w12t": ws[1:].reshape(2 * NF, E).T,
        "bias0": bs[0].reshape(NF, 1),
        "bias12": bs[1:].reshape(1, 2 * NF),
        "dense": a["dense_ctx"].reshape(nb, P, -1).transpose(1, 0, 2),
        "w1": a["W_top1"],
        "b1": a["b_top1"].reshape(-1, P).T,
        "w2": a["W_top2"],
        "b2": a["b_top2"].reshape(-1, P).T,
        "w3": a["W_top3"].reshape(-1, P).T,
        "identity": np.eye(P, dtype=np.float32),
        "sel_out": sel.reshape(P, 2, GR),
    }
    arrays = {k: np.ascontiguousarray(v) for k, v in arrays.items()}
    nc = bacc.Bacc("TRN2", target_bir_lowering=False, num_devices=1)
    args = [nc.dram_tensor(f"in_{k}", v.shape, mybir.dt.from_np(v.dtype), kind="ExternalInput").ap()
            for k, v in arrays.items()]
    out = nc.dram_tensor("out_y", (1, n), F32, kind="ExternalOutput").ap()
    build(nc, args[:NF], *args[NF:], out)
    r = run(nc, [{f"in_{k}": v for k, v in arrays.items()}], core_ids=[0])
    return r.results[0]["out_y"].reshape(n, 1)
```
